# Optimizing a Trainium2 kernel written in Bass

```python
import numpy as np
import jax
import jax.numpy as jnp

def _softmax(x, axis=-1):
    return jax.nn.softmax(x, axis=axis)

def _gelu(x):
    return jax.nn.gelu(x, approximate=True)

def _silu(x):
    return jax.nn.silu(x)

def _sigmoid(x):
    return jax.nn.sigmoid(x)

def _layernorm(x, axis=-1, eps=1e-05):
    m = jnp.mean(x, axis=axis, keepdims=True)
    v = jnp.var(x, axis=axis, keepdims=True)
    return (x - m) / jnp.sqrt(v + eps)

def _scatter_add(tgt, idx, src, axis=0):
    return tgt.at[idx].add(src)

def _segment_sum(src, seg, n):
    return jax.ops.segment_sum(src, seg, n)
kernel_name = 'mk_adaln_d1_jaxref_r8_74aec2'

def setup_inputs(seed: int=0):
    np.random.seed(seed)
    _w = jnp.asarray

    def _L0_attn_setup():
        import jax, jax.numpy as jnp
        import numpy as np
        B, T, E, H = (4, 256, 128, 16)
        S = E // H
        key = jax.random.key(seed)
        ks = jax.random.split(key, 4)
        x = jax.random.normal(ks[0], (B, T, E), dtype=jnp.float32)
        Wk = jax.random.normal(ks[1], (E, E), dtype=jnp.float32) * E ** (-0.5)
        Wq = jax.random.normal(ks[2], (E, E), dtype=jnp.float32) * E ** (-0.5)
        Wo = jax.random.normal(ks[3], (E, E), dtype=jnp.float32) * E ** (-0.5)
        bo = jnp.zeros((E,), dtype=jnp.float32)
        return {'x': x, 'Wk': Wk, 'Wq': Wq, 'Wo': Wo, 'bo': bo}
    _L0_attn_in = _L0_attn_setup()

    def _L0_ffn_setup():
        import jax, jax.numpy as jnp
        import numpy as np
        TOP_K = 2
        key = jax.random.key(seed)
        ks = jax.random.split(key, 6)
        B, T, H, E, F = (2, 256, 128, 8, 512)
        s = 0.02
        return {'hidden_states': jax.random.normal(ks[0], (B, T, H), dtype=jnp.float32), 'router_w': jax.random.normal(ks[1], (E, H), dtype=jnp.float32) * s, 'w1': jax.random.normal(ks[2], (E, F, H), dtype=jnp.float32) * s, 'b1': jax.random.normal(ks[3], (E, F), dtype=jnp.float32) * s, 'w2': jax.random.normal(ks[4], (E, H, F), dtype=jnp.float32) * s, 'b2': jax.random.normal(ks[5], (E, H), dtype=jnp.float32) * s}
    _L0_ffn_in = _L0_ffn_setup()
    _L0_c = _w((lambda *s: np.random.randn(*s).astype(np.float32) * 0.05)(4, 128))
    _L0_wmod = _w((lambda *s: np.random.randn(*s).astype(np.float32) * 0.05)(128, 6 * 128) * 128 ** (-0.5))
    _d = {'L0_attn_x': _L0_attn_in['x'], 'L0_attn_Wk': _L0_attn_in['Wk'], 'L0_attn_Wq': _L0_attn_in['Wq'], 'L0_attn_Wo': _L0_attn_in['Wo'], 'L0_attn_bo': _L0_attn_in['bo'], 'L0_ffn_router_w': _L0_ffn_in['router_w'], 'L0_ffn_w1': _L0_ffn_in['w1'], 'L0_ffn_b1': _L0_ffn_in['b1'], 'L0_ffn_w2': _L0_ffn_in['w2'], 'L0_ffn_b2': _L0_ffn_in['b2'], 'L0_c': _L0_c, 'L0_wmod': _L0_wmod}
    _x0 = _d['L0_attn_x']
    _d['L0_attn_x'] = jax.random.normal(jax.random.fold_in(jax.random.key(seed), 1), (4, 512, 128), dtype=_x0.dtype)
    del _x0
    return _d

def reference(L0_attn_x, L0_attn_Wk, L0_attn_Wq, L0_attn_Wo, L0_attn_bo, L0_ffn_router_w, L0_ffn_w1, L0_ffn_b1, L0_ffn_w2, L0_ffn_b2, L0_c, L0_wmod):

    def _L0_attn_ref(x, Wk, Wq, Wo, bo):
        import jax, jax.numpy as jnp
        import numpy as np
        B, T, E, H = (4, 256, 128, 16)
        S = E // H
        b, t, e = x.shape
        h, s = (H, E // H)
        scale = e ** (-0.25)
        k = (x @ Wk).reshape(b, t, h, s).transpose(0, 2, 1, 3)
        q = (x @ Wq).reshape(b, t, h, s).transpose(0, 2, 1, 3)
        v = (x @ Wk).reshape(b, t, h, s).transpose(0, 2, 1, 3)
        dot = jnp.einsum('bhqd,bhkd->bhqk', q * scale, k * scale)
        attn = jax.nn.softmax(dot, axis=-1)
        out = jnp.einsum('bhqk,bhkd->bhqd', attn, v)
        out = out.transpose(0, 2, 1, 3).reshape(b, t, e)
        return out @ Wo + bo

    def _L0_ffn_ref(hidden_states, router_w, w1, b1, w2, b2):
        import jax, jax.numpy as jnp
        import numpy as np
        TOP_K = 2
        x = hidden_states
        router_logits = jnp.einsum('bth,eh->bte', x, router_w)
        topk_values, topk_indices = jax.lax.top_k(router_logits, TOP_K)
        topk_weights = jax.nn.softmax(topk_values.astype(jnp.float32), axis=-1).astype(x.dtype)
        h1 = jnp.einsum('bth,efh->btef', x, w1) + b1
        h1 = jax.nn.gelu(h1, approximate=False)
        expert_outputs = jnp.einsum('btef,ehf->bteh', h1, w2) + b2
        gather_idx = topk_indices[..., None]
        topk_expert_outputs = jnp.take_along_axis(expert_outputs, gather_idx, axis=2)
        mixed_output = jnp.sum(topk_expert_outputs * topk_weights[..., None], axis=2)
        return mixed_output
    x = L0_attn_x
    mod = (_silu(L0_c) @ L0_wmod).reshape(L0_c.shape[0], 6, 1, -1)
    sa, ca, ga, sb, cb, gb = (mod[:, 0], mod[:, 1], mod[:, 2], mod[:, 3], mod[:, 4], mod[:, 5])
    ga = (2 * (ga >= 0) - 1) * jnp.maximum(jnp.abs(ga), 0.25)
    gb = (2 * (gb >= 0) - 1) * jnp.maximum(jnp.abs(gb), 0.25)
    h = _layernorm(x, axis=-1) * (1 + ca) + sa
    x = x + ga * _L0_attn_ref(h, L0_attn_Wk, L0_attn_Wq, L0_attn_Wo, L0_attn_bo)
    h = _layernorm(x, axis=-1) * (1 + cb) + sb
    x = x + gb * _L0_ffn_ref(h, L0_ffn_router_w, L0_ffn_w1, L0_ffn_b1, L0_ffn_w2, L0_ffn_b2)
    return x

_drawn_inputs = setup_inputs


def setup_inputs(seed=0):
    import zlib

    import numpy as np

    out = dict(_drawn_inputs(seed))
    spreads = {'L0_attn_bo': (0.0, 0.323)}
    factors = {'L0_attn_Wk': 4.654,
     'L0_ffn_router_w': 6.347,
     'L0_ffn_w1': 6.049,
     'L0_ffn_b1': 8.0,
     'L0_ffn_w2': 5.951,
     'L0_ffn_b2': 8.0}
    for name, (base, spread) in spreads.items():
        noise = np.random.default_rng([zlib.crc32(name.encode()), seed]).standard_normal(out[name].shape)
        drawn = base * np.exp(spread * noise) if base else spread * noise
        out[name] = jnp.asarray(drawn.astype(out[name].dtype))
    for name, factor in factors.items():
        out[name] = (out[name] * factor).astype(out[name].dtype)
    return out
```

```python
from contextlib import ExitStack

import concourse.bass as bass
from concourse import mybir
from concourse.alu_op_type import AluOpType as ALU

F32 = mybir.dt.float32
BF16 = mybir.dt.bfloat16
U32 = mybir.dt.uint32
ACT = mybir.ActivationFunctionType
AX_X = mybir.AxisListType.X

P = 128
HEADS = 16
HG = 4
EPS = 1e-5
PARTS = 3
RING = 4


def build(nc, x, cT, wk, wq, wo, bo, router_wT, w1T, b1T, w2T, b2T, wmod, out):
    B, T, E = x.shape
    S = E // HEADS
    TT = T // P
    NT = B * TT
    GB = HEADS // HG
    NX = router_wT.shape[1]
    FF = w1T.shape[1] // NX
    FC = FF // P
    PROD = PARTS * PARTS * S
    MROW = 96
    KEXP = MROW + PARTS
    EXP_SCALE = float(E) ** -0.5
    GROUPS = B * GB
    assert E == P and T == 512 and GB == RING and PROD <= MROW

    with ExitStack() as ctx:
        def sb(name, shape, dt=F32):
            return ctx.enter_context(nc.sbuf_tensor(name, shape, dt))

        def psum(name, shape, dt=F32):
            return ctx.enter_context(nc.psum_tensor(name, shape, dt))

        def sem(name):
            return ctx.enter_context(nc.semaphore(name))

        q_scr = nc.dram_tensor("q_scr", (B, GB, PARTS * S, HG * T), BF16).ap()
        k_scr = nc.dram_tensor("k_scr", (B, GB, PARTS * S, HG * T), BF16).ap()
        wt_scr = nc.dram_tensor("wt_scr", (NX, B * T), F32).ap()

        x_all = sb("x_all", [P, NT, E])
        xres = sb("xres", [P, NT, E])
        v_all = sb("v_all", [P, NT, E])
        attn = sb("attn", [P, NT, E])
        h2T = sb("h2T", [P, B, T])
        wkb = sb("wkb", [P, E])
        wqb = sb("wqb", [P, E])
        wob = sb("wob", [P, E])
        rwb = sb("rwb", [P, NX])
        wmb = sb("wmb", [P, 6 * E])
        bob = sb("bob", [P, E])
        b1b = sb("b1b", [P, NX * FC])
        b2b = sb("b2b", [P, NX])
        ctb = sb("ctb", [P, B])
        sig = sb("sig", [P, B])
        silu = sb("silu", [P, B])
        silu_w = sb("silu_w", [P, B, P])
        modc = sb("modc", [P, 6, B])
        gate_row = sb("gate_row", [P, 2, B, E])
        gtmp = sb("gtmp", [P, 2, B, E])
        ident = sb("ident", [P, P])
        identb = sb("identb", [P, P], BF16)
        stats = sb("stats", [P, TT, 6])
        mv = sb("mv", [P, TT, 2])
        vareps = sb("vareps", [P, TT])
        rstd = sb("rstd", [P, TT])
        mhalf = sb("mhalf", [P, TT])
        xn = sb("xn", [P, TT, E])
        hT = sb("hT", [P, T])
        parts = [sb(f"parts_{n}", [P, PARTS, T], BF16) for n in "qk"]
        rest = [sb(f"rest_{n}", [P, T]) for n in "qk"]
        qs = [sb(f"qs{r}", [P, HG, T], BF16) for r in range(RING)]
        ks = [sb(f"ks{r}", [P, HG, T], BF16) for r in range(RING)]
        mcol = sb("mcol", [P, HG * TT])
        mres = sb("mres", [P, HG * TT])
        mneg = [sb(f"mneg{r}", [P, PARTS, HG * TT], BF16) for r in range(2)]
        mrow = [sb(f"mrow{r}", [PARTS * HG * TT, P], BF16) for r in range(2)]
        vcur = [sb(f"vcur{r}", [P, TT, HG, 32]) for r in range(2)]
        probs = sb("probs", [P, TT, HG, T])
        o_sb = sb("o_sb", [P, T])
        rden = sb("rden", [P, TT, HG])
        aT = sb("aT", [P, T])
        ytmp = sb("ytmp", [P, TT, E])
        top = sb("top", [P, TT, 8])
        topi = sb("topi", [P, TT, 8], U32)
        topf = sb("topf", [P, TT, 2])
        wexp = sb("wexp", [P, TT])
        wden = sb("wden", [P, TT])
        wtop = sb("wtop", [P, 2, TT])
        iota_e = sb("iota_e", [P, NX])
        wmask = sb("wmask", [P, 2, TT, NX])
        w_te = sb("w_te", [P, TT, NX])
        logits = sb("logits", [P, TT, NX])
        wT_sb = sb("wT_sb", [NX, T])

        mx = [psum(f"mx{r}", [P, 2, T]) for r in range(2)]
        sc = [psum(f"sc{r}", [P, T]) for r in range(2)]
        pv = psum("pv", [P, T])
        tr = psum("tr", [P, TT, P])
        tr_m = tr[:, 0, :].bitcast(BF16)

        x_in = [sem(f"x_in{b}") for b in range(B)]; w_in = sem("w_in"); ones_set = sem("ones_set")
        pool_k = sem("pool_k"); consts = sem("consts")
        sig_r = sem("sig_r"); silu_r = sem("silu_r"); mod_ps = sem("mod_ps"); mod_r = sem("mod_r")
        gate_ps = sem("gate_ps"); gate_r = sem("gate_r"); dchain = sem("dchain")
        stat_r = sem("stat_r"); rstd_r = sem("rstd_r"); xn_r = sem("xn_r"); xnT_ps = sem("xnT_ps")
        hT_r = sem("hT_r"); q_ps = sem("q_ps"); k_ps = sem("k_ps"); v_ps = sem("v_ps")
        part1 = [sem(f"part1_{n}") for n in "qk"]
        rest_r = [sem(f"rest_{n}") for n in "qk"]
        part2 = [sem(f"part2_{n}") for n in "qk"]
        part3 = [sem(f"part3_{n}") for n in "qk"]
        scr_w = [sem(f"scr_w_{n}") for n in "qk"]
        v_r = sem("v_r")
        ld = [sem(f"ld{r}") for r in range(RING)]
        ldm = [sem(f"ldm{r}") for r in range(RING)]
        mx_ready = sem("mx_ready"); mx_used = sem("mx_used"); mneg_r = sem("mneg_r")
        mT_ps = sem("mT_ps"); mrow_r = sem("mrow_r")
        sc_ready = sem("sc_ready"); p_ready = sem("p_ready"); vcur_r = sem("vcur_r")
        pv_done = sem("pv_done"); o_r = sem("o_r"); oT_ps = sem("oT_ps"); den_r = sem("den_r")
        attn_r = sem("attn_r")
        xres_r = sem("xres_r")
        aT_ps = sem("aT_ps"); aT_r = sem("aT_r"); y_ps = sem("y_ps"); x2_r = sem("x2_r")
        stat2_r = sem("stat2_r"); rstd2_r = sem("rstd2_r"); xn2_r = sem("xn2_r")
        xn2T_ps = sem("xn2T_ps"); h2T_r = sem("h2T_r"); lg_ps = sem("lg_ps"); top_r = sem("top_r")
        wexp_r = sem("wexp_r"); w_r = sem("w_r"); wT_ps = sem("wT_ps"); wT_r = sem("wT_r")
        wt_w = sem("wt_w"); wb_in = sem("wb_in")
        ew_in = [sem(f"ew_in{r}") for r in range(2)]
        h_ps = sem("h_ps"); g_r = sem("g_r"); y2_ps = sem("y2_ps"); ymul = sem("ymul")
        yacc_r = sem("yacc_r"); fT_ps = sem("fT_ps"); fin_r = sem("fin_r"); fmul = sem("fmul")
        out_w = sem("out_w")



        flat = probs[:].rearrange("p a h t -> p (a h t)")
        at = [0]

        def room(n):
            at[0] += n
            return flat[:, at[0] - n:at[0]]
        g_sb = [room(FC * T) for _ in range(2)]
        yacc = room(B * T)
        w1e = [room(FF) for _ in range(2)]
        w2e = [room(FC * E) for _ in range(2)]
        wbc = [sb(f"wbc{r}", [P, B * T])[:] for r in range(2)]
        ys = sb("ys", [P, 2, T])

        def x_tiles(b):
            return x_all[:, bass.ds(b * TT, TT), :]

        block = ctx.enter_context(nc.Block())
        N_W = 11 * 16

        @block.sync
        def _(sp):
            for b in range(B):
                sp.dma_start(x_all[:, b * TT:(b + 1) * TT, :],
                             x[b].rearrange("(t p) e -> p t e", p=P)).then_inc(x_in[b], 16)
                if b == 0:
                    for dst, src in ((ctb[:], cT), (wmb[:], wmod), (wqb[:], wq), (wkb[:], wk),
                                     (wob[:], wo), (rwb[:], router_wT),
                                     (bob[:], bo.broadcast_to((P, E))), (b1b[:], b1T), (b2b[:], b2T)):
                        sp.dma_start(dst, src).then_inc(w_in, 16)
            for b in range(B):
                for n, scr in ((0, q_scr), (1, k_scr)):
                    sp.wait_ge(part3[n], b + 1)
                    for g in range(GB):
                        src = parts[n][HG * S * g:HG * S * (g + 1), :, :]
                        for h in range(HG):
                            sp.dma_start(
                                scr[b, g].rearrange("(i s) (h t) -> s i h t", s=S, h=HG)[:, :, h, :],
                                src[S * h:S * (h + 1)]).then_inc(scr_w[n], 16)

            def load(b, g):
                for n in range(2):
                    sp.wait_ge(scr_w[n], 16 * GB * HG * (b + 1))
                G = b * GB + g
                if G >= RING:
                    sp.wait_ge(sc_ready, HG * TT * (G - RING + 1))
                for i in range(PARTS):
                    rows = slice(PARTS * S * i, PARTS * S * (i + 1))
                    sp.dma_start(ks[g][rows, :, :].rearrange("p h t -> p (h t)"),
                                 k_scr[b, g]).then_inc(ld[g], 16)
                    for j in range(PARTS):
                        rows = slice(PARTS * S * i + S * j, PARTS * S * i + S * (j + 1))
                        sp.dma_start(qs[g][rows, :, :].rearrange("p h t -> p (h t)"),
                                     q_scr[b, g, S * i:S * (i + 1), :]).then_inc(ld[g], 16)

            def load_max(b, g):
                G = b * GB + g
                sp.wait_ge(mrow_r, G + 1)
                n = HG * TT
                for i in range(PARTS):
                    sp.dma_start(qs[g][MROW + i:MROW + i + 1, :, :].rearrange("o h (q t) -> o (h q) t", t=P),
                                 mrow[g % 2][n * i:n * (i + 1), :]).then_inc(ldm[g], 16)

            for r in range(RING):
                if r == 0:
                    sp.wait_ge(ones_set, 1)
                load(0, r)
            for G in range(GROUPS):
                load_max(G // GB, G % GB)
                if G >= 2 and G + 2 < GROUPS:
                    load((G + 2) // GB, (G + 2) % GB)

            for b in range(B):
                sp.wait_ge(wT_r, b + 1)
                sp.dma_start(wt_scr[:, T * b:T * (b + 1)], wT_sb[:]).then_inc(wt_w, 16)
                sp.wait_ge(wt_w, 16 * (b + 1))
            sp.wait_ge(attn_r, GROUPS)
            for e in range(NX):
                if e >= 2:
                    sp.wait_ge(y2_ps, B * (e - 1))
                sp.dma_start(w1e[e % 2], w1T[:, FF * e:FF * (e + 1)]).then_inc(ew_in[e % 2], 16)
                sp.dma_start(w2e[e % 2], w2T[:, FC * E * e:FC * E * (e + 1)]).then_inc(ew_in[e % 2], 16)
                if e >= 2:
                    sp.wait_ge(ymul, B * (e - 1))
                sp.dma_start(wbc[e % 2], wt_scr[e:e + 1, :].broadcast_to((P, B * T))).then_inc(ew_in[e % 2], 16)
            for b in range(B):
                sp.wait_ge(fin_r, b + 1)
                sp.dma_start(out[b].rearrange("(t p) e -> p t e", p=P),
                             xres[:, b * TT:(b + 1) * TT, :]).then_inc(out_w, 16)
            sp.wait_ge(out_w, 16 * B)

        @block.gpsimd
        def _(pool):
            pool.memset(ident[:], 0.0).then_inc(pool_k, 1)
            pool.memset(identb[:], 0.0).then_inc(pool_k, 1)
            pool.memset(mhalf[:], -0.5).then_inc(consts, 1)
            pool.wait_ge(pool_k, 2)
            for m in (ident, identb):
                pool.affine_select(out=m[:], in_=m[:], compare_op=ALU.not_equal, fill=1.0, base=0,
                                   pattern=[[-1, P]], channel_multiplier=1).then_inc(consts, 1)
            pool.iota(iota_e[:], pattern=[[1, NX]], base=0, channel_multiplier=0,
                      allow_small_or_imprecise_dtypes=True).then_inc(consts, 1)
            for r in range(2):
                pool.memset(vcur[r][:], 0.0).then_inc(pool_k, 1)
            pool.wait_ge(pool_k, 4)
            for r in range(2):
                pool.memset(vcur[r][:, :, :, S:S + 1], 1.0).then_inc(pool_k, 1)

            def rstd_of(ready, n, done):
                pool.wait_ge(ready, n)
                pool.tensor_tensor(rstd[:], vareps[:], mhalf[:], ALU.pow).then_inc(done, 1)

            for b in range(B):
                rstd_of(stat_r, b + 1, rstd_r)
            pool.wait_ge(gate_r, 1)
            for b in range(B):
                pool.wait_ge(x_in[b], 16)
                pool.tensor_tensor(ytmp[:, 0, :], gate_row[:, 0, b, :], bob[:], ALU.mult).then_inc(xres_r, 1)
                pool.wait_ge(xres_r, 2 * b + 1)
                pool.tensor_tensor(xres[:, b * TT:(b + 1) * TT, :], x_all[:, b * TT:(b + 1) * TT, :],
                                   ytmp[:, 0:1, :].broadcast_to((P, TT, E)), ALU.add).then_inc(xres_r, 1)
                pool.wait_ge(xres_r, 2 * b + 2)
            pool.wait_ge(pool_k, 6)
            for G in range(GROUPS):
                b, g = G // GB, G % GB
                pool.wait_ge(v_r, b + 1)
                if G >= 2:
                    pool.wait_ge(pv_done, TT * (G - 1))
                pool.tensor_copy(vcur[G % 2][:, :, :, 0:S],
                                 v_all[:, b * TT:(b + 1) * TT, HG * S * g:HG * S * (g + 1)]
                                 .rearrange("p k (h s) -> p k h s", h=HG)).then_inc(vcur_r, 1)
            for b in range(B):
                rstd_of(stat2_r, b + 1, rstd2_r)

        @block.scalar
        def _(act):
            act.wait_ge(w_in, 9 * 16)
            act.activation(sig[:], ctb[:], ACT.Exp, scale=-1.0).then_inc(sig_r, 1)
            act.wait_ge(mod_r, 1)
            for b in range(B):
                act.wait_ge(xnT_ps, b + 1)
                if b >= 1:
                    act.wait_ge(v_ps, b)
                act.activation(hT[:], tr[:].rearrange("p t e -> p (t e)"), ACT.Identity,
                               scale=modc[:, 1, b:b + 1], bias=modc[:, 0, b:b + 1]).then_inc(hT_r, 1)
                for n, ready in ((0, q_ps), (1, k_ps)):
                    act.wait_ge(ready, b + 1)
                    if b >= 1:
                        act.wait_ge(scr_w[n], 16 * GB * HG * b)
                    act.copy(parts[n][:, 0, :], mx[n][:, 0, :]).then_inc(part1[n], 1)
                for n in range(2):
                    act.wait_ge(rest_r[n], b + 1)
                    act.copy(parts[n][:, 1, :], rest[n][:]).then_inc(part2[n], 1)

            def m_rows(G):
                act.wait_ge(mT_ps, G + 1)
                if G >= 2:
                    act.wait_ge(ldm[(G - 2) % RING], 16 * PARTS * ((G - 2) // GB + 1))
                act.copy(mrow[G % 2][:], tr_m[0:PARTS * HG * TT, 0:P]).then_inc(mrow_r, 1)

            def o_copy(G):
                act.wait_ge(pv_done, TT * (G + 1))
                if G >= 1:
                    act.wait_ge(oT_ps, G)
                act.copy(o_sb[:], pv[:]).then_inc(o_r, 1)

            m_rows(0)
            for G in range(GROUPS):
                for n in range(HG * TT):
                    if n == 4 and G + 1 < GROUPS:
                        m_rows(G + 1)
                    if n == 5 and G >= 1:
                        o_copy(G - 1)
                    kt, j = n // HG, n % HG
                    act.wait_ge(sc_ready, HG * TT * G + n + 1)
                    if G >= 1 and j == 0:
                        act.wait_ge(pv_done, TT * (G - 1) + kt + 1)
                    act.activation(probs[:, kt, j, :], sc[n % 2][:], ACT.Exp,
                                   scale=EXP_SCALE).then_inc(p_ready, 1)
            o_copy(GROUPS - 1)

            for b in range(B):
                act.wait_ge(aT_ps, b + 1)
                if b >= 1:
                    act.wait_ge(y_ps, b)
                act.copy(aT[:], tr[:].rearrange("p t e -> p (t e)")).then_inc(aT_r, 1)
                act.wait_ge(xn2T_ps, b + 1)
                act.activation(h2T[:, b, :], tr[:].rearrange("p t e -> p (t e)"), ACT.Identity,
                               scale=modc[:, 4, b:b + 1], bias=modc[:, 3, b:b + 1]).then_inc(h2T_r, 1)
                act.wait_ge(top_r, b + 1)
                act.activation(wexp[:], wexp[:], ACT.Exp).then_inc(wexp_r, 1)

            hb = [mx[0][:, 0, :], mx[0][:, 1, :], mx[1][:, 0, :], mx[1][:, 1, :]]
            for i in range(NX * B):
                e = i // B
                for f in range(FC):
                    act.wait_ge(h_ps, FC * i + f + 1)
                    if i >= 2:
                        act.wait_ge(y2_ps, i - 1)
                    act.activation(g_sb[i % 2][:, f * T:(f + 1) * T], hb[f], ACT.Gelu,
                                   bias=b1b[:, e * FC + f:e * FC + f + 1]).then_inc(g_r, 1)

        @block.vector
        def _(dve):
            chain = [0]

            def link(ins):
                chain[0] += 1
                ins.then_inc(dchain, 1)
                dve.wait_ge(dchain, chain[0])

            for r in range(RING):
                link(dve.memset(ks[r][:], 1.0))
                link(dve.memset(ks[r][64:96], 0.0))
                last = dve.memset(qs[r][:], 0.0)
            last.then_inc(ones_set, 1)
            dve.wait_ge(sig_r, 1)
            link(dve.tensor_scalar(sig[:], sig[:], 1.0, None, ALU.add))
            link(dve.reciprocal(sig[:], sig[:]))
            link(dve.tensor_tensor(silu[:], sig[:], ctb[:], ALU.mult))
            link(dve.tensor_copy(silu_w[:], silu[:].rearrange("p (b o) -> p b o", o=1).broadcast_to((P, B, P))))
            dve.sem_inc(silu_r, 1)
            dve.wait_ge(mod_ps, 1)
            link(dve.tensor_copy(modc[:], pv[:, 0:6 * B].rearrange("p (m b) -> p m b", b=B)))
            for m in (1, 4):
                link(dve.tensor_scalar(modc[:, m, :], modc[:, m, :], 1.0, None, ALU.add))
            dve.sem_inc(mod_r, 1)
            dve.wait_ge(gate_ps, 1)
            for n in range(2):
                row = gate_row[:, n].rearrange("p b e -> p (b e)")
                tmp = gtmp[:, n].rearrange("p b e -> p (b e)")
                link(dve.tensor_scalar(row, sc[n][:], 0.0, 2.0, ALU.is_ge, ALU.mult))
                link(dve.tensor_scalar(tmp, sc[n][:], -1.0, 0.25, ALU.mult, ALU.max))
                link(dve.tensor_tensor(tmp, tmp, sc[n][:], ALU.max))
                link(dve.scalar_tensor_tensor(row, row, -1.0, tmp, ALU.add, ALU.mult))
            dve.sem_inc(gate_r, 1)

            def layer_norm(src, b, stats_done, rstd_done, out_done, free, n_free):
                for t in range(TT):
                    dve.bn_stats(stats[:, t, :], src[:, b * TT + t, :]).then_inc(dchain, 1)
                chain[0] += TT
                dve.wait_ge(dchain, chain[0])
                for t in range(TT):
                    dve.bn_aggr(mv[:, t, :], stats[:, t, :]).then_inc(dchain, 1)
                chain[0] += TT
                dve.wait_ge(dchain, chain[0])
                dve.tensor_scalar(vareps[:], mv[:, :, 1], EPS, None, ALU.add).then_inc(stats_done, 1)
                dve.wait_ge(rstd_done, b + 1)
                if n_free:
                    dve.wait_ge(free, n_free)
                for t in range(TT):
                    last = dve.tensor_scalar(xn[:, t, :], src[:, b * TT + t, :], mv[:, t, 0:1],
                                             rstd[:, t:t + 1], ALU.subtract, ALU.mult)
                last.then_inc(out_done, 1)

            for b in range(B):
                dve.wait_ge(x_in[b], 16)
                layer_norm(x_all, b, stat_r, rstd_r, xn_r, xnT_ps, b)
                for n in range(2):
                    dve.wait_ge(part1[n], b + 1)
                    dve.tensor_tensor(rest[n][:], mx[n][:, 0, :], parts[n][:, 0, :], ALU.subtract).then_inc(rest_r[n], 1)
                dve.wait_ge(v_ps, b + 1)
                dve.tensor_copy(v_all[:, b * TT:(b + 1) * TT, :].rearrange("p t e -> p (t e)"), sc[0][:]).then_inc(v_r, 1)
                for n in range(2):
                    dve.wait_ge(part2[n], b + 1)
                    dve.tensor_tensor(parts[n][:, 2, :], rest[n][:], parts[n][:, 1, :], ALU.subtract).then_inc(part3[n], 1)

            def max_unit(G, u):
                dve.wait_ge(mx_ready, 2 * HG * G + u + 1)
                if u == 0 and G >= 1:
                    dve.wait_ge(mneg_r, G)
                dve.tensor_reduce(mcol[:, 2 * u:2 * u + 2], mx[u % 2][:], AX_X, ALU.max).then_inc(mx_used, 1)

            def max_split(G):
                dve.wait_ge(mx_used, 2 * HG * (G + 1))
                if G >= 2:
                    dve.wait_ge(mT_ps, G - 1)
                m = mneg[G % 2]
                link(dve.tensor_scalar(m[:, 0, :], mcol[:], -1.0, None, ALU.mult))
                link(dve.scalar_tensor_tensor(mres[:], mcol[:], -1.0, m[:, 0, :], ALU.mult, ALU.subtract))
                link(dve.tensor_copy(m[:, 1, :], mres[:]))
                dve.tensor_tensor(m[:, 2, :], mres[:], m[:, 1, :], ALU.subtract).then_inc(mneg_r, 1)

            def normalise(G):
                b, g = G // GB, G % GB
                dve.wait_ge(oT_ps, G + 1)
                o = tr[:].rearrange("p q (h c) -> p q h c", c=32)
                dve.reciprocal(rden[:].rearrange("p q (h o) -> p q h o", o=1), o[:, :, :, S:S + 1]).then_inc(den_r, 1)
                dve.wait_ge(den_r, G + 1)
                dst = attn[:, b * TT:(b + 1) * TT, HG * S * g:HG * S * (g + 1)].rearrange("p q (h s) -> p q h s", s=S)
                dve.tensor_tensor(dst, o[:, :, :, 0:S],
                                  rden[:].rearrange("p q (h o) -> p q h o", o=1).broadcast_to((P, TT, HG, S)),
                                  ALU.mult).then_inc(attn_r, 1)

            for slot in range(-2, GROUPS):
                for s in range(2 * HG):
                    if slot + 2 < GROUPS:
                        max_unit(slot + 2, s)
                    if s == 4 and slot >= 1:
                        normalise(slot - 1)
                if slot + 2 < GROUPS:
                    max_split(slot + 2)
            normalise(GROUPS - 1)

            for b in range(B):
                dve.wait_ge(y_ps, b + 1)
                dve.wait_ge(xres_r, 2 * B)
                tiles = slice(b * TT, (b + 1) * TT)
                link(dve.tensor_tensor(ytmp[:], sc[0][:].rearrange("p (t e) -> p t e", e=E),
                                       gate_row[:, 0, b:b + 1, :].broadcast_to((P, TT, E)), ALU.mult))
                link(dve.tensor_tensor(xres[:, tiles, :], xres[:, tiles, :], ytmp[:], ALU.add))
                layer_norm(xres, b, stat2_r, rstd2_r, xn2_r, xn2T_ps, b)
                dve.wait_ge(lg_ps, b + 1)
                link(dve.tensor_copy(logits[:], sc[1][:, 0:TT * NX].rearrange("p (t e) -> p t e", e=NX)))
                for t in range(TT):
                    link(dve.max(top[:, t, :], logits[:, t, :]))
                    link(dve.max_index(topi[:, t, :], top[:, t, :], logits[:, t, :]))
                link(dve.tensor_copy(topf[:], topi[:, :, 0:2]))
                dve.tensor_tensor(wexp[:], top[:, :, 1], top[:, :, 0], ALU.subtract).then_inc(top_r, 1)
                dve.wait_ge(wexp_r, b + 1)
                link(dve.tensor_scalar(wden[:], wexp[:], 1.0, None, ALU.add))
                link(dve.reciprocal(wtop[:, 0, :], wden[:]))
                link(dve.tensor_tensor(wtop[:, 1, :], wexp[:], wtop[:, 0, :], ALU.mult))
                for t in range(TT):
                    for n in range(2):
                        dve.tensor_scalar(wmask[:, n, t, :], iota_e[:], topf[:, t, n:n + 1],
                                          wtop[:, n, t:t + 1], ALU.is_equal, ALU.mult).then_inc(dchain, 1)
                chain[0] += 2 * TT
                dve.wait_ge(dchain, chain[0])
                if b:
                    dve.wait_ge(wT_ps, b)
                dve.tensor_tensor(w_te[:], wmask[:, 0], wmask[:, 1], ALU.add).then_inc(w_r, 1)
                dve.wait_ge(wT_ps, b + 1)
                if b:
                    dve.wait_ge(wt_w, 16 * b)
                dve.tensor_copy(wT_sb[:], pv[0:NX, :]).then_inc(wT_r, 1)

            for i in range(NX * B):
                e, b = i // B, i % B
                dve.wait_ge(y2_ps, i + 1)
                dve.wait_ge(ew_in[e % 2], 48 * (e // 2 + 1))
                y = yacc[:, T * b:T * (b + 1)] if e == 0 else ys[:, 0, :]
                link(dve.scalar_tensor_tensor(y, sc[i % 2][:], b2b[:, e:e + 1],
                                              wbc[e % 2][:, T * b:T * (b + 1)], ALU.add, ALU.mult))
                dve.sem_inc(ymul, 1)
                if e:
                    link(dve.tensor_tensor(yacc[:, T * b:T * (b + 1)], yacc[:, T * b:T * (b + 1)], y, ALU.add))
                dve.sem_inc(yacc_r, 1)
            for b in range(B):
                tiles = slice(b * TT, (b + 1) * TT)
                dve.wait_ge(fT_ps, b + 1)
                if b:
                    dve.wait_ge(fin_r, b)
                link(dve.tensor_tensor(ytmp[:], tr[:], gate_row[:, 1, b:b + 1, :].broadcast_to((P, TT, E)), ALU.mult))
                dve.sem_inc(fmul, 1)
                dve.tensor_tensor(xres[:, tiles, :], xres[:, tiles, :], ytmp[:], ALU.add).then_inc(fin_r, 1)

        @block.tensor
        def _(pe):
            pe.wait_ge(silu_r, 1)
            for m in range(6):
                last = pe.matmul(pv[:, B * m:B * (m + 1)], wmb[:, E * m:E * (m + 1)], silu[:], start=True, stop=True)
            last.then_inc(mod_ps, 1)
            for n, m in ((0, 2), (1, 5)):
                for b in range(B):
                    last = pe.matmul(sc[n][:, E * b:E * (b + 1)], silu_w[:, b, :], wmb[:, E * m:E * (m + 1)],
                                     start=True, stop=True)
            last.then_inc(gate_ps, 1)
            pe.wait_ge(consts, 4)
            for b in range(B):
                pe.wait_ge(xn_r, b + 1)
                if b:
                    pe.wait_ge(hT_r, b)
                for t in range(TT):
                    last = pe.transpose(tr[:, t, :], xn[:, t, :], ident[:])
                last.then_inc(xnT_ps, 1)
                pe.wait_ge(hT_r, b + 1)
                for n, w, ready in ((0, wqb, q_ps), (1, wkb, k_ps)):
                    if b:
                        pe.wait_ge(rest_r[n], b)
                    pe.matmul(mx[n][:, 0, :], w[:], hT[:], start=True, stop=True).then_inc(ready, 1)
                pe.wait_ge(gate_r, 1)
                if b:
                    pe.wait_ge(v_r, b)
                for t in range(TT):
                    last = pe.matmul(sc[0][:, P * t:P * (t + 1)], hT[:, P * t:P * (t + 1)], wkb[:],
                                     start=True, stop=True)
                last.then_inc(v_ps, 1)

            def max_unit(G, u):
                b, g = G // GB, G % GB
                if u == 0:
                    pe.wait_ge(ld[g], 16 * (PARTS + PARTS * PARTS) * (b + 1))
                if 2 * HG * G + u >= 2:
                    pe.wait_ge(mx_used, 2 * HG * G + u - 1)
                j = u // 2
                for c in range(2):
                    qt = 2 * (u % 2) + c
                    last = pe.matmul(mx[u % 2][:, c, :], qs[g][0:MROW, j, P * qt:P * (qt + 1)],
                                     ks[g][0:MROW, j, :], start=True, stop=True)
                last.then_inc(mx_ready, 1)

            def score(G, n):
                b, g = G // GB, G % GB
                kt, j = n // HG, n % HG
                if n == 0:
                    pe.wait_ge(ldm[g], 16 * PARTS * (b + 1))
                if HG * TT * G + n >= 2:
                    pe.wait_ge(p_ready, HG * TT * G + n - 1)
                pe.matmul(sc[n % 2][:], ks[g][0:KEXP, j, P * kt:P * (kt + 1)], qs[g][0:KEXP, j, :],
                          start=True, stop=True).then_inc(sc_ready, 1)

            def weigh(G, kt):
                pe.wait_ge(p_ready, HG * TT * G + HG * (kt + 1))
                if kt == 0:
                    pe.wait_ge(vcur_r, G + 1)
                    if G:
                        pe.wait_ge(o_r, G)
                for j in range(HG):
                    last = pe.matmul(pv[32 * j:32 * (j + 1), :], vcur[G % 2][:, kt, j, :], probs[:, kt, j, :],
                                     start=kt == 0, stop=kt == TT - 1, skip_group_check=True)
                last.then_inc(pv_done, 1)

            def max_transpose(G):
                pe.wait_ge(mneg_r, G + 1)
                if G >= 3:
                    pe.wait_ge(attn_r, G - 2)
                if G:
                    pe.wait_ge(mrow_r, G)
                pe.transpose(tr_m[0:PARTS * HG * TT, 0:P], mneg[G % 2][:].rearrange("p i n -> p (i n)"),
                             identb[:]).then_inc(mT_ps, 1)

            def out_transpose(G):
                pe.wait_ge(o_r, G + 1)
                if G:
                    pe.wait_ge(attn_r, G)
                pe.wait_ge(mrow_r, min(G + 3, GROUPS))
                for t in range(TT):
                    last = pe.transpose(tr[:, t, :], o_sb[:, P * t:P * (t + 1)], ident[:])
                last.then_inc(oT_ps, 1)

            for slot in range(-2, GROUPS):
                for s in range(2 * HG):
                    if slot + 2 < GROUPS:
                        if slot == -2 and s == 0:
                            for n in range(2):
                                pe.wait_ge(part3[n], B)
                            pe.wait_ge(v_r, B)
                        max_unit(slot + 2, s)
                    if slot >= 0:
                        score(slot, 2 * s)
                        score(slot, 2 * s + 1)
                    if s == 1 and slot >= 1:
                        weigh(slot - 1, TT - 1)
                    if s == 2 and slot >= -1 and slot + 1 < GROUPS:
                        max_transpose(slot + 1)
                    if s == 4 and slot >= 1:
                        out_transpose(slot - 1)
                    if slot >= 0 and s >= 3 and s % 2:
                        weigh(slot, (s - 3) // 2)
            weigh(GROUPS - 1, TT - 1)
            out_transpose(GROUPS - 1)

            for b in range(B):
                pe.wait_ge(attn_r, GROUPS)
                if b:
                    pe.wait_ge(h2T_r, b)
                for t in range(TT):
                    last = pe.transpose(tr[:, t, :], attn[:, b * TT + t, :], ident[:])
                last.then_inc(aT_ps, 1)
                pe.wait_ge(aT_r, b + 1)
                if b:
                    pe.wait_ge(xn2_r, b)
                for t in range(TT):
                    last = pe.matmul(sc[0][:, P * t:P * (t + 1)], aT[:, P * t:P * (t + 1)], wob[:],
                                     start=True, stop=True)
                last.then_inc(y_ps, 1)
                pe.wait_ge(xn2_r, b + 1)
                for t in range(TT):
                    last = pe.transpose(tr[:, t, :], xn[:, t, :], ident[:])
                last.then_inc(xn2T_ps, 1)
                pe.wait_ge(h2T_r, b + 1)
                if b:
                    pe.wait_ge(top_r, b)
                for t in range(TT):
                    last = pe.matmul(sc[1][:, NX * t:NX * (t + 1)], h2T[:, b, P * t:P * (t + 1)], rwb[:],
                                     start=True, stop=True)
                last.then_inc(lg_ps, 1)
                pe.wait_ge(w_r, b + 1)
                if b:
                    pe.wait_ge(wT_r, b)
                for t in range(TT):
                    last = pe.transpose(pv[0:NX, P * t:P * (t + 1)], w_te[:, t, :], ident[:])
                last.then_inc(wT_ps, 1)

            hb = [mx[0][:, 0, :], mx[0][:, 1, :], mx[1][:, 0, :], mx[1][:, 1, :]]

            def expand(i):
                e, b = i // B, i % B
                pe.wait_ge(ew_in[e % 2], 48 * (e // 2 + 1))
                for f in range(FC):
                    if i:
                        pe.wait_ge(g_r, FC * (i - 1) + f + 1)
                    pe.matmul(hb[f], w1e[e % 2][:, P * f:P * (f + 1)], h2T[:, b, :],
                              start=True, stop=True).then_inc(h_ps, 1)

            def contract(i):
                e = i // B
                if i >= 2:
                    pe.wait_ge(yacc_r, i - 1)
                for f in range(FC):
                    pe.wait_ge(g_r, FC * i + f + 1)
                    last = pe.matmul(sc[i % 2][:], w2e[e % 2][:, E * f:E * (f + 1)], g_sb[i % 2][:, f * T:(f + 1) * T],
                                     start=f == 0, stop=f == FC - 1)
                last.then_inc(y2_ps, 1)

            for i in range(NX * B + 1):
                if i < NX * B:
                    expand(i)
                if i:
                    contract(i - 1)
            for b in range(B):
                pe.wait_ge(yacc_r, NX * B)
                if b:
                    pe.wait_ge(fmul, b)
                for t in range(TT):
                    last = pe.transpose(tr[:, t, :], yacc[:, T * b + P * t:T * b + P * (t + 1)], ident[:])
                last.then_inc(fT_ps, 1)


_ARGS = ["x", "cT", "wk", "wq", "wo", "bo", "router_wT", "w1T", "b1T", "w2T", "b2T", "wmod"]


def kernel(L0_attn_x, L0_attn_Wk, L0_attn_Wq, L0_attn_Wo, L0_attn_bo, L0_ffn_router_w, L0_ffn_w1,
           L0_ffn_b1, L0_ffn_w2, L0_ffn_b2, L0_c, L0_wmod):
    import numpy as np
    import concourse.bacc as bacc
    from concourse.bass_utils import run_bass_kernel_spmd

    n_x, ff, e = L0_ffn_w1.shape
    w1 = np.asarray(L0_ffn_w1)
    w2 = np.asarray(L0_ffn_w2)
    laid = {
        "x": np.asarray(L0_attn_x),
        "cT": np.asarray(L0_c).T,
        "wk": np.asarray(L0_attn_Wk), "wq": np.asarray(L0_attn_Wq), "wo": np.asarray(L0_attn_Wo),
        "bo": np.asarray(L0_attn_bo).reshape(1, e),
        "router_wT": np.asarray(L0_ffn_router_w).T,
        "w1T": w1.transpose(2, 0, 1).reshape(e, n_x * ff),
        "b1T": np.asarray(L0_ffn_b1).reshape(n_x * ff // 128, 128).T,
        "w2T": w2.transpose(0, 2, 1).reshape(n_x, ff // 128, 128, e).transpose(2, 0, 1, 3)
                 .reshape(128, n_x * ff // 128 * e),
        "b2T": np.asarray(L0_ffn_b2).T,
        "wmod": np.asarray(L0_wmod),
    }
    laid = {k: np.ascontiguousarray(v) for k, v in laid.items()}
    nc = bacc.Bacc("TRN2", target_bir_lowering=False, num_devices=1)
    aps = [nc.dram_tensor(f"in_{k}", laid[k].shape, mybir.dt.from_np(laid[k].dtype), kind="ExternalInput").ap()
           for k in _ARGS]
    out = nc.dram_tensor("out_x", laid["x"].shape, F32, kind="ExternalOutput").ap()
    build(nc, *aps, out)
    r = run_bass_kernel_spmd(nc, [{f"in_{k}": laid[k] for k in _ARGS}], core_ids=[0])
    return r.results[0]["out_x"]
```

```python
from contextlib import ExitStack

import concourse.bass as bass
from concourse import mybir
from concourse.alu_op_type import AluOpType as ALU

F32 = mybir.dt.float32
BF16 = mybir.dt.bfloat16
U32 = mybir.dt.uint32
ACT = mybir.ActivationFunctionType
AX_X = mybir.AxisListType.X

P = 128
HEADS = 16
HG = 4
EPS = 1e-5
PARTS = 3
RING = 4
ONES_PAIR = 1 + 0x3F80 / 2.0 ** 23


def build(nc, x, cT, wk, wqp, wkp, wo, bo, router_wT, w1b, w2T, b2, wmod, out):
    B, T, E = x.shape
    S = E // HEADS
    TT = T // P
    NT = B * TT
    GB = HEADS // HG
    NX = router_wT.shape[1]
    FC = w2T.shape[1] // (NX * E)
    FF = FC * P
    WB = FF + FC
    TOK = B * T
    PROD = PARTS * PARTS * S
    MROW = 96
    KEXP = MROW + PARTS
    EXP_SCALE = float(E) ** -0.5
    GROUPS = B * GB
    UNITS = 2 * HG
    NS = HG * TT
    LDG = 16 * (1 + PARTS)
    BLOCKS = (2 * TOK - NX) // P + NX
    REGION = TOK // P
    TAB = NX * REGION + BLOCKS
    LOADS = 8
    PAD = 2 * TOK
    assert E == P and T == 512 and GB == RING and PROD <= MROW and TOK & (TOK - 1) == 0

    with ExitStack() as ctx:
        def sb(name, shape, dt=F32):
            return ctx.enter_context(nc.sbuf_tensor(name, shape, dt))

        def psum(name, shape, dt=F32):
            return ctx.enter_context(nc.psum_tensor(name, shape, dt))

        def sem(name):
            return ctx.enter_context(nc.semaphore(name))

        q_scr = nc.dram_tensor("q_scr", (B, GB, PARTS, S, HG * T), BF16).ap()
        k_scr = nc.dram_tensor("k_scr", (B, GB, PARTS, S, HG * T), BF16).ap()
        h2_scr = nc.dram_tensor("h2_scr", (TOK, E), F32).ap()
        table = nc.dram_tensor("table", (TAB * P, 2), F32).ap()
        y_scr = nc.dram_tensor("y_scr", (2 * TOK, E), F32).ap()

        x_all = sb("x_all", [P, NT, E])
        v_all = sb("v_all", [P, NT, E])
        attn = sb("attn", [P, NT, E])
        w1_all = sb("w1_all", [P, NX * WB])
        w2_all = sb("w2_all", [P, NX * FC * E])
        wkb = sb("wkb", [P, E])
        wqpb = sb("wqpb", [P, E])
        wkpb = sb("wkpb", [P, E])
        wob = sb("wob", [P, E])
        rwb = sb("rwb", [P, NX])
        wmb = sb("wmb", [P, 6 * E])
        bob = sb("bob", [P, E])
        ctb = sb("ctb", [P, B])
        sig = sb("sig", [P, B])
        silu = sb("silu", [P, B])
        silu_w = sb("silu_w", [P, B, P])
        modc = sb("modc", [P, 2, B])
        mod_row = sb("mod_row", [P, 4, B, E])
        ga_row, gb_row, cb_row, sb_row = (mod_row[:, n] for n in range(4))
        gsign = sb("gsign", [P, B * E])
        gabs = sb("gabs", [P, B * E])
        gabo = sb("gabo", [P, E])
        ident = sb("ident", [P, P])
        identb = sb("identb", [P, P], BF16)
        before = sb("before", [P, P], BF16)
        onesb = sb("onesb", [P, P], BF16)
        stats = sb("stats", [P, TT, 6])
        mv = sb("mv", [P, TT, 2])
        vareps = sb("vareps", [P, TT])
        rstd = sb("rstd", [P, TT])
        mhalf = sb("mhalf", [P, TT])
        xn = sb("xn", [P, TT, E])
        hT = sb("hT", [P, T])
        parts = [sb(f"parts_{n}", [P, PARTS, T], BF16) for n in "qk"]
        rest = [sb(f"rest_{n}", [P, T]) for n in "qk"]
        qs = [sb(f"qs{r}", [P, HG, T], BF16) for r in range(RING)]
        ks = [sb(f"ks{r}", [P, HG, T], BF16) for r in range(RING)]
        mcol = sb("mcol", [P, NS])
        mres = sb("mres", [P, NS])
        mneg = [sb(f"mneg{r}", [P, PARTS, NS], BF16) for r in range(2)]
        mrow = [sb(f"mrow{r}", [PARTS * NS, P], BF16) for r in range(2)]
        vcur = [sb(f"vcur{r}", [P, TT, HG, 32]) for r in range(2)]
        probs = sb("probs", [P, TT, HG, T])
        o_sb = sb("o_sb", [P, T])
        rden = sb("rden", [P, TT, HG])
        aT = sb("aT", [P, T])
        ytmp = sb("ytmp", [P, TT, E])
        xn2 = sb("xn2", [P, TT, E])
        h2 = sb("h2", [P, TT, E])
        h2T = sb("h2T", [P, T])
        top = sb("top", [P, TT, 8])
        topi = sb("topi", [P, TT, 8], U32)
        topf = sb("topf", [P, 2, TT])
        wexp = sb("wexp", [P, TT])
        wden = sb("wden", [P, TT])
        logits = sb("logits", [P, TT, NX])
        iota_e = sb("iota_e", [P, NX])
        hot = sb("hot", [P, 2, TT, NX])
        hots = sb("hots", [P, TT, NX], BF16)
        run = sb("run", [P, TT + 1, NX])
        slots = sb("slots", [P, TT, NX])
        hslots = sb("hslots", [P, 2 * TT, NX])
        posf = sb("posf", [P, 2 * TT])
        pos = [sb(f"pos{r}", [P, 2 * TT], U32) for r in range(2)]
        entry = sb("entry", [P, 2, NT, 2])
        tab0 = sb("tab0", [P, TAB, 2])
        base_e = sb("base_e", [P, NX])
        cnt = sb("cnt", [P, NX])
        cntu = sb("cntu", [P, NX], U32)
        nblk = sb("nblk", [P, NX])
        ones_e = sb("ones_e", [P, NX])
        cum = sb("cum", [P, NX])
        skip = sb("skip", [P, NX])
        part_i = sb("part_i", [P, 1])
        passed = sb("passed", [P, NX])
        startf = sb("startf", [P, 1])
        startu = sb("startu", [P, 1], U32)
        iota_b = sb("iota_b", [P, BLOCKS])
        over = sb("over", [P, BLOCKS, NX])
        eidf = sb("eidf", [P, BLOCKS])
        eid = sb("eid", [P, BLOCKS], U32)
        tabT = sb("tabT", [BLOCKS, P, 2])
        dest = sb("dest", [P, BLOCKS], U32)
        srcs = sb("srcs", [P, BLOCKS], U32)
        wslot = sb("wslot", [P, BLOCKS])
        b2_row = sb("b2_row", [P, NX * E])
        XR = 6
        WR = 4
        xb = [sb(f"xb{r}", [P, E]) for r in range(XR)]
        xbT = [sb(f"xbT{r}", [P, P]) for r in range(2)]
        w1_blk = [qs[r][:].rearrange("p h t -> p (h t)").bitcast(F32)[:, 0:WB] for r in range(WR)]
        g_sb = [ks[r][:].rearrange("p h t -> p (h t)").bitcast(F32)[:, 0:FF] for r in range(2)]
        yc = [sb(f"yc{r}", [P, E]) for r in range(2)]
        yb = [sb(f"yb{r}", [P, E]) for r in range(XR)]
        y_room = probs[:].rearrange("p a h t -> p (a h t)").rearrange("p (n t e) -> p n t e", t=TT, e=E)

        def y_of(b, n):
            return y_room[:, 2 * b + n]

        mx = [psum(f"mx{r}", [P, 2, T]) for r in range(2)]
        sc = [psum(f"sc{r}", [P, T]) for r in range(2)]
        pv = psum("pv", [P, T])
        tr = psum("tr", [P, TT, P])
        tr_flat = tr[:].rearrange("p t e -> p (t e)")
        tr_m = tr[:, 0, :].bitcast(BF16)
        xp = [tr[:, 0, :], pv[:, 0:P]]

        x_in = [sem(f"x_in{b}") for b in range(B)]
        wa_in = sem("wa_in"); wb_in = sem("wb_in"); wc_in = sem("wc_in"); we_in = sem("we_in")
        pads_r = sem("pads_r"); vpad_r = sem("vpad_r")
        pool_k = sem("pool_k"); consts = sem("consts"); dchain = sem("dchain"); pchain = sem("pchain")
        sig_r = sem("sig_r"); silu_r = sem("silu_r"); mod_ps = sem("mod_ps"); mod_r = sem("mod_r")
        row_ps = sem("row_ps"); row_r = sem("row_r"); gate_r = sem("gate_r")
        stat_r = sem("stat_r"); xn_r = sem("xn_r"); xnT_ps = sem("xnT_ps")
        hT_r = sem("hT_r"); q_ps = sem("q_ps"); k_ps = sem("k_ps"); v_ps = sem("v_ps")
        qk_ps = [q_ps, k_ps]
        part1 = [sem(f"part1_{n}") for n in "qk"]
        rest_r = [sem(f"rest_{n}") for n in "qk"]
        part2 = [sem(f"part2_{n}") for n in "qk"]
        part3 = [sem(f"part3_{n}") for n in "qk"]
        scr_w = [sem(f"scr_w_{n}") for n in "qk"]
        v_r = sem("v_r"); lg_r = sem("lg_r"); px_r = sem("px_r"); tabz = sem("tabz")
        ld = [sem(f"ld{r}") for r in range(RING)]
        ldm = [sem(f"ldm{r}") for r in range(RING)]
        mx_ready = sem("mx_ready"); mx_used = sem("mx_used"); mneg_r = sem("mneg_r")
        mT_ps = sem("mT_ps"); mrow_r = sem("mrow_r")
        sc_ready = sem("sc_ready"); p_ready = sem("p_ready"); vcur_r = sem("vcur_r")
        pv_done = sem("pv_done"); o_r = sem("o_r"); oT_ps = sem("oT_ps"); attn_r = sem("attn_r")
        aT_ps = sem("aT_ps"); aT_r = sem("aT_r"); y_ps = sem("y_ps"); ytmp_r = sem("ytmp_r")
        x2_r = sem("x2_r"); stat2_r = sem("stat2_r"); h2_r = sem("h2_r"); h2T_ps = sem("h2T_ps")
        h2T_r = sem("h2T_r"); lg_ps = sem("lg_ps"); top_r = sem("top_r"); wexp_r = sem("wexp_r")
        hot_r = sem("hot_r"); px_ps = sem("px_ps"); pos_r = sem("pos_r")
        h2_w = sem("h2_w"); tab_w = sem("tab_w"); ent_w = [sem(f"ent_w{r}") for r in range(2)]
        start_r = sem("start_r"); eid_r = sem("eid_r"); tabT_in = sem("tabT_in"); tb_ps = sem("tb_ps")
        dest_r = sem("dest_r")
        xb_in = [sem(f"xb_in{r}") for r in range(XR)]
        xbT_ps = sem("xbT_ps"); xbT_r = sem("xbT_r"); h_ps = sem("h_ps"); w1_r = sem("w1_r"); g_r = sem("g_r")
        yb_ps = sem("yb_ps"); yc_r = sem("yc_r"); yb_r = sem("yb_r")
        y_w = [sem(f"y_w{r}") for r in range(XR)]
        y_in = [sem(f"y_in{b}") for b in range(B)]
        ysum_r = sem("ysum_r"); fin_r = sem("fin_r"); out_w = sem("out_w")

        def extras(G, s):
            b, g = G // GB, G % GB
            todo = []
            if s == 2 and 0 <= G + 1 < GROUPS:
                todo.append(("m", G + 1))
            if s == 4 and G >= 1:
                todo.append(("o", G - 1))
            c = b + 2 if g == 3 else b + 1
            if G >= -1 and 1 <= c < B:
                todo += [(kind, c) for kind in {(3, 0): ("xnT",), (3, 3): ("q",), (3, 6): ("k",),
                                                (0, 0): ("v",)}.get((g, s), ())]
            if b >= 1:
                todo += [(kind, b - 1) for kind in {(0, 6): ("aT",), (1, 0): ("y",), (2, 0): ("h2T",),
                                                    (2, 1): ("lg",), (2, 6): ("px",)}.get((g, s), ())]
            return todo

        order = [("xnT", 0)]
        for G in range(-2, GROUPS):
            for s in range(UNITS):
                order += extras(G, s)
        order += [("o", GROUPS - 1), ("aT", B - 1), ("y", B - 1), ("h2T", B - 1), ("lg", B - 1), ("px", B - 1),
                  ("tb", 0)]
        turn = {use: n for n, use in enumerate(order)}

        block = ctx.enter_context(nc.Block())

        @block.sync
        def _(sp):
            sp.dma_start(x_all[:, 0:TT, :], x[0].rearrange("(t p) e -> p t e", p=P)).then_inc(x_in[0], 16)
            for dst, src in ((ctb[:], cT), (wmb[:], wmod)):
                sp.dma_start(dst, src).then_inc(wa_in, 16)
            for dst, src in ((wqpb[:], wqp), (wkpb[:], wkp), (wkb[:], wk)):
                sp.dma_start(dst, src).then_inc(wb_in, 16)
            for b in range(1, B):
                sp.dma_start(x_all[:, b * TT:(b + 1) * TT, :],
                             x[b].rearrange("(t p) e -> p t e", p=P)).then_inc(x_in[b], 16)
            for dst, src in ((wob[:], wo), (rwb[:], router_wT), (bob[:], bo.broadcast_to((P, E)))):
                sp.dma_start(dst, src).then_inc(wc_in, 16)

            def store_parts(n, c):
                sp.wait_ge(part3[n], c + 1)
                scr = (q_scr, k_scr)[n]
                for i in range(PARTS):
                    sp.dma_start(scr[c, :, i].rearrange("g s (h t) -> g (s h) t", t=T),
                                 parts[n][:, i, :]).then_inc(scr_w[n], 16)

            def load(G):
                b, g = G // GB, G % GB
                for n in range(2):
                    sp.wait_ge(scr_w[n], 16 * PARTS * (b + 1))
                if G >= RING:
                    sp.wait_ge(sc_ready, NS * (G - RING + 1))
                ksrc = k_scr[b, g].rearrange("(o j) s n -> o (j s) n", o=1)
                sp.dma_start(ks[g][0:PROD].rearrange("p h t -> p (h t)"),
                             ksrc.broadcast_to((PARTS, PARTS * S, HG * T))).then_inc(ld[g], 16)
                for i in range(PARTS):
                    qsrc = q_scr[b, g, i:i + 1].broadcast_to((PARTS, S, HG * T))
                    sp.dma_start(qs[g][PARTS * S * i:PARTS * S * (i + 1)].rearrange("p h t -> p (h t)"),
                                 qsrc).then_inc(ld[g], 16)

            def load_max(G):
                g = G % GB
                sp.wait_ge(mrow_r, G + 1)
                sp.dma_start(qs[g][MROW:KEXP].rearrange("i h (q t) -> i (h q) t", t=P),
                             mrow[G % 2][:]).then_inc(ldm[g], 16)

            def store_h2(d):
                sp.wait_ge(h2_r, d + 1)
                sp.dma_start(h2_scr[T * d:T * (d + 1), :].rearrange("(t p) e -> p t e", p=P),
                             h2[:]).then_inc(h2_w, 16)

            for n in range(2):
                store_parts(n, 0)
            sp.wait_ge(pads_r, 1)
            for G in range(RING):
                load(G)
            for G in range(-1, GROUPS):
                g = G % GB
                if 1 <= G and G + 3 < GROUPS:
                    load(G + 3)
                if G + 1 < GROUPS:
                    load_max(G + 1)
                if g == 3 and (G + 5) // GB < B:
                    store_parts(0, (G + 5) // GB)
                if g == 0 and (G + 4) // GB < B:
                    store_parts(1, (G + 4) // GB)
                if g == 2 and G >= GB:
                    store_h2(G // GB - 1)
                if G == 0:
                    sp.wait_ge(tabz, 1)
                    sp.dma_start(table.rearrange("(r p) c -> p r c", p=P), tab0[:]).then_inc(tab_w, 16)
                if 2 <= G < 2 + NX:
                    e = G - 2
                    sp.dma_start(w1_all[:, WB * e:WB * (e + 1)], w1b[:, WB * e:WB * (e + 1)]).then_inc(we_in, 16)
                    sp.dma_start(w2_all[:, FC * E * e:FC * E * (e + 1)],
                                 w2T[:, FC * E * e:FC * E * (e + 1)]).then_inc(we_in, 16)
                if G == 2 + NX:
                    sp.dma_start(b2_row[:], b2.broadcast_to((P, NX * E))).then_inc(we_in, 16)
            store_h2(B - 1)
            for r in range(XR):
                sp.wait_ge(y_w[r], 16 * len(range(r, BLOCKS, XR)))
            for b in range(B):
                for n in range(2):
                    sp.dma_start(y_of(b, n),
                                 y_scr[TOK * n + T * b:TOK * n + T * (b + 1), :].rearrange("(t p) e -> p t e", p=P)
                                 ).then_inc(y_in[b], 16)
            for b in range(B):
                sp.wait_ge(fin_r, b + 1)
                sp.dma_start(out[b].rearrange("(t p) e -> p t e", p=P),
                             x_all[:, b * TT:(b + 1) * TT, :]).then_inc(out_w, 16)
            sp.wait_ge(out_w, 16 * B)

        @block.gpsimd
        def _(pool):
            chain = [0]

            def link(ins):
                chain[0] += 1
                ins.then_inc(pchain, 1)
                pool.wait_ge(pchain, chain[0])

            pool.memset(mhalf[:], -0.5).then_inc(consts, 1)
            pool.memset(ident[:], 0.0).then_inc(pool_k, 1)
            pool.memset(identb[:], 0.0).then_inc(pool_k, 1)
            pool.memset(onesb[:], 1.0).then_inc(consts, 1)
            pool.memset(before[:], 1.0).then_inc(pool_k, 1)
            pool.wait_ge(pool_k, 3)
            for m in (ident, identb):
                pool.affine_select(out=m[:], in_=m[:], compare_op=ALU.not_equal, fill=1.0, base=0,
                                   pattern=[[-1, P]], channel_multiplier=1).then_inc(consts, 1)

            def layer_norm(src, b, ready, n, dst, done):
                pool.wait_ge(ready, n)
                link(pool.tensor_tensor(rstd[:], vareps[:], mhalf[:], ALU.pow))
                bc = (P, TT, E)
                link(pool.tensor_tensor(dst[:], src[:, b * TT:(b + 1) * TT, :], mv[:, :, 0:1].broadcast_to(bc), ALU.subtract))
                last = pool.tensor_tensor(dst[:], dst[:], rstd[:].rearrange("p (t o) -> p t o", o=1).broadcast_to(bc), ALU.mult)
                if done is None:
                    link(last)
                else:
                    last.then_inc(done, 1)

            def norm1(c):
                if c:
                    pool.wait_ge(xnT_ps, c)
                layer_norm(x_all, c, stat_r, c + 1, xn, xn_r)

            norm1(0)
            pool.affine_select(out=before[:], in_=before[:], compare_op=ALU.is_gt, fill=0.0, base=0,
                               pattern=[[1, P]], channel_multiplier=-1).then_inc(consts, 1)
            for r in range(2):
                link(pool.memset(vcur[r][:], 0.0))
                pool.memset(vcur[r][:, :, :, S:S + 1], 1.0).then_inc(vpad_r, 1)
            pool.iota(iota_e[:], pattern=[[1, NX]], base=0, channel_multiplier=0,
                      allow_small_or_imprecise_dtypes=True).then_inc(consts, 1)
            pool.iota(iota_b[:], pattern=[[1, BLOCKS]], base=0, channel_multiplier=0,
                      allow_small_or_imprecise_dtypes=True).then_inc(consts, 1)
            pool.iota(part_i[:], pattern=[[0, 1]], base=0, channel_multiplier=1,
                      allow_small_or_imprecise_dtypes=True).then_inc(consts, 1)
            E_ = entry[:].rearrange("p n t c -> p (n t) c")
            pool.iota(E_[:, :, 0], pattern=[[P, 2 * NT]], base=0, channel_multiplier=1,
                      allow_small_or_imprecise_dtypes=True).then_inc(consts, 1)
            pool.iota(base_e[:], pattern=[[TOK, NX]], base=0, channel_multiplier=0,
                      allow_small_or_imprecise_dtypes=True).then_inc(consts, 1)
            pool.memset(ones_e[:], 1.0).then_inc(consts, 1)

            def v_group(G):
                b, g = G // GB, G % GB
                pool.wait_ge(v_r, b + 1)
                pool.wait_ge(vpad_r, 2)
                if G >= 2:
                    pool.wait_ge(pv_done, TT * (G - 1))
                pool.tensor_copy(vcur[G % 2][:, :, :, 0:S],
                                 v_all[:, b * TT:(b + 1) * TT, HG * S * g:HG * S * (g + 1)]
                                 .rearrange("p k (h s) -> p k h s", h=HG)).then_inc(vcur_r, 1)

            def part_3(n, c):
                pool.wait_ge(part2[n], c + 1)
                pool.tensor_tensor(parts[n][:, 2, :], rest[n][:], parts[n][:, 1, :], ALU.subtract).then_inc(part3[n], 1)

            def bias_x(d):
                pool.wait_ge(wc_in, 48)
                pool.wait_ge(gate_r, 1)
                link(pool.tensor_tensor(gabo[:], ga_row[:, d, :], bob[:], ALU.mult))
                xd = x_all[:, d * TT:(d + 1) * TT, :]
                link(pool.tensor_tensor(xd, xd, gabo[:].rearrange("p (o e) -> p o e", o=1).broadcast_to((P, TT, E)), ALU.add))

            def residual(d):
                pool.wait_ge(ytmp_r, d + 1)
                xd = x_all[:, d * TT:(d + 1) * TT, :]
                link(pool.tensor_tensor(xd, xd, ytmp[:], ALU.add))
                pool.sem_inc(x2_r, 1)

            def norm2(d):
                if d:
                    pool.wait_ge(h2_w, 16 * d)
                    pool.wait_ge(h2T_ps, d)
                layer_norm(x_all, d, stat2_r, d + 1, xn2, None)
                bc = (P, TT, E)
                link(pool.tensor_tensor(xn2[:], xn2[:], cb_row[:, d:d + 1, :].broadcast_to(bc), ALU.mult))
                pool.tensor_tensor(h2[:], xn2[:], sb_row[:, d:d + 1, :].broadcast_to(bc), ALU.add).then_inc(h2_r, 1)

            def enter(d):
                pool.wait_ge(tab_w, 16)
                pool.wait_ge(consts, 11)
                pool.wait_ge(pos_r, d + 1)
                for n in range(2):
                    for t in range(TT):
                        pool.indirect_dma_start(
                            table, bass.IndirectOffsetOnAxis(ap=pos[d % 2][:, n * TT + t:n * TT + t + 1], axis=0),
                            entry[:, n, d * TT + t, :], None).then_inc(ent_w[d % 2], 16)

            for n in range(2):
                part_3(n, 0)
            norm1(1)
            for G in range(-2, GROUPS):
                b, g = G // GB, G % GB
                if g == 0 and G >= 0 and b + 1 < B:
                    part_3(1, b + 1)
                if G + 1 < GROUPS and G >= -1:
                    v_group(G + 1)
                if g == 0 and G >= 0 and b + 2 < B:
                    norm1(b + 2)
                if g == 0 and b >= 1:
                    bias_x(b - 1)
                if g == 1 and b >= 1:
                    residual(b - 1)
                    norm2(b - 1)
                if g == 3 and b >= 1:
                    enter(b - 1)
                if g == 3 and b + 2 < B:
                    part_3(0, b + 2)
            bias_x(B - 1)
            residual(B - 1)
            norm2(B - 1)
            enter(B - 1)
            for r in range(2):
                pool.wait_ge(ent_w[r], 16 * 2 * TT * len(range(r, B, 2)))
            pool.wait_ge(start_r, 1)
            pool.indirect_dma_start(tabT[:].rearrange("r p c -> r (p c)"), None,
                                    table.rearrange("(r p) c -> r (p c)", p=P),
                                    bass.IndirectOffsetOnAxis(ap=startu[0:BLOCKS, :], axis=0)).then_inc(tabT_in, 16)
            pool.wait_ge(h2_w, 16 * B)
            pool.wait_ge(dest_r, 1)
            for i in range(BLOCKS + XR):
                if i < BLOCKS:
                    if i >= XR:
                        pool.wait_ge(xbT_ps, i - XR + 1)
                    pool.indirect_dma_start(xb[i % XR][:], None, h2_scr,
                                            bass.IndirectOffsetOnAxis(ap=srcs[:, i:i + 1], axis=0)).then_inc(xb_in[i % XR], 16)
                if i >= XR:
                    j = i - XR
                    pool.wait_ge(yb_r, j + 1)
                    pool.indirect_dma_start(y_scr, bass.IndirectOffsetOnAxis(ap=dest[:, j:j + 1], axis=0), yb[j % XR][:],
                                            None, bounds_check=2 * TOK - 1, oob_is_err=False).then_inc(y_w[j % XR], 16)
            for b in range(B):
                pool.wait_ge(y_in[b], 32)
                pool.tensor_tensor(y_of(b, 0), y_of(b, 0), y_of(b, 1), ALU.add).then_inc(ysum_r, 1)

        @block.scalar
        def _(act):
            act.wait_ge(wa_in, 32)
            act.activation(sig[:], ctb[:], ACT.Exp, scale=-1.0).then_inc(sig_r, 1)

            def modulate(c):
                act.wait_ge(xnT_ps, c + 1)
                if c:
                    act.wait_ge(v_ps, c)
                act.activation(hT[:], tr_flat, ACT.Identity, scale=modc[:, 1, c:c + 1],
                               bias=modc[:, 0, c:c + 1]).then_inc(hT_r, 1)

            def first_part(n, c, src):
                act.wait_ge(qk_ps[n], c + 1)
                if c:
                    act.wait_ge(scr_w[n], 16 * PARTS * c)
                act.copy(parts[n][:, 0, :], src).then_inc(part1[n], 1)

            def second_part(n, c):
                act.wait_ge(rest_r[n], c + 1)
                act.copy(parts[n][:, 1, :], rest[n][:]).then_inc(part2[n], 1)

            def v_copy(c, src):
                act.wait_ge(v_ps, c + 1)
                act.copy(v_all[:, c * TT:(c + 1) * TT, :].rearrange("p t e -> p (t e)"), src).then_inc(v_r, 1)

            def m_rows(G):
                act.wait_ge(mT_ps, G + 1)
                if G >= 2:
                    act.wait_ge(ldm[(G - 2) % RING], 16 * ((G - 2) // GB + 1))
                act.copy(mrow[G % 2][:], tr_m[0:PARTS * NS, 0:P]).then_inc(mrow_r, 1)

            def o_copy(G):
                act.wait_ge(pv_done, TT * (G + 1))
                if G >= 1:
                    act.wait_ge(oT_ps, G)
                act.copy(o_sb[:], pv[:]).then_inc(o_r, 1)

            def a_copy(d):
                act.wait_ge(aT_ps, d + 1)
                if d:
                    act.wait_ge(y_ps, d)
                act.copy(aT[:], tr_flat).then_inc(aT_r, 1)

            def h2_copy(d):
                act.wait_ge(h2T_ps, d + 1)
                if d:
                    act.wait_ge(lg_ps, d)
                act.copy(h2T[:], tr_flat).then_inc(h2T_r, 1)

            def top_exp(d):
                act.wait_ge(top_r, d + 1)
                act.activation(wexp[:], wexp[:], ACT.Exp).then_inc(wexp_r, 1)

            act.wait_ge(mod_r, 1)
            modulate(0)
            for n in range(2):
                first_part(n, 0, mx[n][:, 0, :])
            for n in range(2):
                second_part(n, 0)
            v_copy(0, sc[0][:])
            act.wait_ge(row_ps, 1)
            for n, bank in enumerate((mx[0][:, 1, :], mx[1][:, 1, :], sc[1][:], pv[:])):
                act.copy(mod_row[:, n].rearrange("p b e -> p (b e)"), bank).then_inc(row_r, 1)

            take_act = {"xnT": modulate, "q": lambda c: first_part(0, c, tr_flat), "k": lambda c: first_part(1, c, tr_flat),
                        "v": lambda c: v_copy(c, tr_flat), "m": m_rows, "aT": a_copy, "h2T": h2_copy}

            def exp(G, n):
                kt, j = n // HG, n % HG
                act.wait_ge(sc_ready, NS * G + n + 1)
                if G >= 1 and j == 0:
                    act.wait_ge(pv_done, TT * (G - 1) + kt + 1)
                act.activation(probs[:, kt, j, :], sc[n % 2][:], ACT.Exp, scale=EXP_SCALE).then_inc(p_ready, 1)

            for G in range(-2, GROUPS):
                b, g = G // GB, G % GB
                for s in range(UNITS):
                    if G >= 0:
                        exp(G, 2 * s)
                        exp(G, 2 * s + 1)
                    if s == 0 and G >= 1:
                        o_copy(G - 1)
                    for kind, n in extras(G, s):
                        if kind in take_act:
                            take_act[kind](n)
                    if g == 3 and s == 4 and b + 2 < B:
                        second_part(0, b + 2)
                    if g == 3 and s == 7 and b + 2 < B:
                        second_part(1, b + 2)
                    if g == 2 and s == 3 and b >= 1:
                        top_exp(b - 1)
            o_copy(GROUPS - 1)
            a_copy(B - 1)
            h2_copy(B - 1)
            top_exp(B - 1)

            for i in range(BLOCKS + 1):
                if i < BLOCKS:
                    act.wait_ge(h_ps, i + 1)
                    if i >= 2:
                        act.wait_ge(yb_ps, i - 1)
                    for f in range(FC):
                        last = act.activation(g_sb[i % 2][:, P * f:P * (f + 1)], mx[0][:, i % 2, P * f:P * (f + 1)],
                                              ACT.Gelu, bias=w1_blk[i % WR][:, FF + f:FF + f + 1])
                    last.then_inc(g_r, 1)
                if i >= 1:
                    j = i - 1
                    act.wait_ge(yc_r, j + 1)
                    if j >= XR:
                        act.wait_ge(y_w[j % XR], 16 * (j // XR))
                    act.activation(yb[j % XR][:], yc[j % 2][:], ACT.Copy,
                                   scale=wslot[:, j:j + 1]).then_inc(yb_r, 1)

        @block.vector
        def _(dve):
            chain = [0]

            def link(ins, n=1):
                chain[0] += n
                ins.then_inc(dchain, 1)
                dve.wait_ge(dchain, chain[0])

            def mean_var(src, b, done):
                for t in range(TT - 1):
                    dve.bn_stats(stats[:, t, :], src[:, b * TT + t, :]).then_inc(dchain, 1)
                link(dve.bn_stats(stats[:, TT - 1, :], src[:, b * TT + TT - 1, :]), TT)
                for t in range(TT - 1):
                    dve.bn_aggr(mv[:, t, :], stats[:, t, :]).then_inc(dchain, 1)
                link(dve.bn_aggr(mv[:, TT - 1, :], stats[:, TT - 1, :]), TT)
                dve.tensor_scalar(vareps[:], mv[:, :, 1], EPS, None, ALU.add).then_inc(done, 1)

            for r in range(RING):
                dve.memset(ks[r][64:96].rearrange("p h t -> p (h t)").bitcast(F32), 0.0)
                dve.memset(ks[r][96:128].rearrange("p h t -> p (h t)").bitcast(F32), ONES_PAIR)
                last = dve.memset(qs[r][64:128].rearrange("p h t -> p (h t)").bitcast(F32), 0.0)
                if r == 0:
                    dve.wait_ge(sig_r, 1)
                    link(dve.tensor_scalar(sig[:], sig[:], 1.0, None, ALU.add))
                    link(dve.reciprocal(sig[:], sig[:]))
                    link(dve.tensor_tensor(silu[:], sig[:], ctb[:], ALU.mult))
                    link(dve.tensor_copy(silu_w[:], silu[:].rearrange("p (b o) -> p b o", o=1).broadcast_to((P, B, P))))
                    dve.sem_inc(silu_r, 1)
                    dve.wait_ge(x_in[0], 16)
                    mean_var(x_all, 0, stat_r)
                if r == 1:
                    dve.wait_ge(mod_ps, 1)
                    link(dve.tensor_copy(modc[:], pv[:, 0:2 * B].rearrange("p (m b) -> p m b", b=B)))
                    link(dve.tensor_scalar(modc[:, 1, :], modc[:, 1, :], 1.0, None, ALU.add))
                    dve.sem_inc(mod_r, 1)
            last.then_inc(pads_r, 1)

            def rest_part(n, c, src, in_tr):
                dve.wait_ge(part1[n], c + 1)
                if c:
                    dve.wait_ge(part3[n], c)
                link(dve.tensor_tensor(rest[n][:], src, parts[n][:, 0, :], ALU.subtract))
                dve.sem_inc(rest_r[n], 1)

            for n in range(2):
                rest_part(n, 0, mx[n][:, 0, :], False)

            def empty_table():
                link(dve.memset(tab0[:, :, 0], float(PAD)))
                dve.memset(tab0[:, :, 1], 0.0).then_inc(tabz, 1)

            def max_unit(G, u):
                dve.wait_ge(mx_ready, UNITS * G + u + 1)
                if u == 0 and G >= 1:
                    dve.wait_ge(mneg_r, G)
                dve.tensor_reduce(mcol[:, 2 * u:2 * u + 2], mx[u % 2][:], AX_X, ALU.max).then_inc(mx_used, 1)

            def max_split(G):
                dve.wait_ge(mx_used, UNITS * (G + 1))
                if G >= 2:
                    dve.wait_ge(mT_ps, G - 1)
                m = mneg[G % 2]
                link(dve.tensor_scalar(m[:, 0, :], mcol[:], -1.0, None, ALU.mult))
                link(dve.scalar_tensor_tensor(mres[:], mcol[:], -1.0, m[:, 0, :], ALU.mult, ALU.subtract))
                link(dve.tensor_copy(m[:, 1, :], mres[:]))
                dve.tensor_tensor(m[:, 2, :], mres[:], m[:, 1, :], ALU.subtract).then_inc(mneg_r, 1)

            def normalise(G):
                b, g = G // GB, G % GB
                dve.wait_ge(oT_ps, G + 1)
                o = tr[:].rearrange("p q (h c) -> p q h c", c=32)
                rd = rden[:].rearrange("p q (h o) -> p q h o", o=1)
                link(dve.reciprocal(rd, o[:, :, :, S:S + 1]))
                dst = attn[:, b * TT:(b + 1) * TT, HG * S * g:HG * S * (g + 1)].rearrange("p q (h s) -> p q h s", s=S)
                dve.tensor_tensor(dst, o[:, :, :, 0:S], rd.broadcast_to((P, TT, HG, S)), ALU.mult).then_inc(attn_r, 1)

            def gate_y(d):
                dve.wait_ge(y_ps, d + 1)
                dve.wait_ge(gate_r, 1)
                if d:
                    dve.wait_ge(x2_r, d)
                dve.tensor_tensor(ytmp[:], tr[:], ga_row[:, d:d + 1, :].broadcast_to((P, TT, E)),
                                  ALU.mult).then_inc(ytmp_r, 1)

            def stats_2(d):
                dve.wait_ge(x2_r, d + 1)
                dve.wait_ge(xn_r, B)
                if d:
                    dve.wait_ge(h2_r, d)
                mean_var(x_all, d, stat2_r)

            def stats_1(c):
                dve.wait_ge(x_in[c], 16)
                dve.wait_ge(xn_r, c)
                mean_var(x_all, c, stat_r)

            def choose(d):
                dve.wait_ge(lg_ps, d + 1)
                dve.wait_ge(consts, 11)
                link(dve.tensor_copy(logits[:], tr_flat[:, 0:TT * NX].rearrange("p (t e) -> p t e", e=NX)))
                dve.sem_inc(lg_r, 1)
                for t in range(TT):
                    ins = dve.max(top[:, t, :], logits[:, t, :])
                    link(ins, 1) if t == TT - 1 else ins.then_inc(dchain, 1)
                    if t < TT - 1:
                        chain[0] += 1
                for t in range(TT):
                    ins = dve.max_index(topi[:, t, :], top[:, t, :], logits[:, t, :])
                    link(ins, 1) if t == TT - 1 else ins.then_inc(dchain, 1)
                    if t < TT - 1:
                        chain[0] += 1
                dve.tensor_tensor(wexp[:], top[:, :, 1], top[:, :, 0], ALU.subtract).then_inc(top_r, 1)
                link(dve.tensor_copy(topf[:], topi[:, :, 0:2].rearrange("p t n -> p n t")))
                for n in range(2):
                    ins = dve.tensor_tensor(hot[:, n], iota_e[:].rearrange("p (o e) -> p o e", o=1).broadcast_to((P, TT, NX)),
                                            topf[:, n, :].rearrange("p (t o) -> p t o", o=1).broadcast_to((P, TT, NX)),
                                            ALU.is_equal)
                    if n:
                        link(ins)
                    else:
                        chain[0] += 1
                        ins.then_inc(dchain, 1)
                if d:
                    dve.wait_ge(px_ps, d)
                dve.tensor_tensor(hots[:], hot[:, 0], hot[:, 1], ALU.add).then_inc(hot_r, 1)

            def weights(d):
                dve.wait_ge(wexp_r, d + 1)
                w = [entry[:, n, d * TT:(d + 1) * TT, 1] for n in range(2)]
                link(dve.tensor_scalar(wden[:], wexp[:], 1.0, None, ALU.add))
                link(dve.reciprocal(w[0], wden[:]))
                link(dve.tensor_tensor(w[1], wexp[:], w[0], ALU.mult))

            def place(d):
                dve.wait_ge(px_ps, d + 1)
                if d == 0:
                    dve.wait_ge(consts, 10)
                    link(dve.tensor_copy(run[:, 0, :], base_e[:]))
                else:
                    link(dve.tensor_copy(run[:, 0, :], run[:, TT, :]))
                for t in range(TT):
                    link(dve.tensor_tensor(run[:, t + 1, :], tr_flat[:, (TT + t) * NX:(TT + t + 1) * NX], run[:, t, :], ALU.add))
                link(dve.tensor_tensor(slots[:], tr_flat[:, 0:TT * NX].rearrange("p (t e) -> p t e", e=NX), run[:, 0:TT, :], ALU.add))
                dve.sem_inc(px_r, 1)
                for n in range(2):
                    link(dve.tensor_tensor(hslots[:, n * TT:(n + 1) * TT, :], hot[:, n], slots[:], ALU.mult))
                link(dve.tensor_reduce(posf[:], hslots[:], AX_X, ALU.add))
                if d >= 2:
                    dve.wait_ge(ent_w[d % 2], 16 * 2 * TT * (d // 2))
                dve.tensor_copy(pos[d % 2][:], posf[:]).then_inc(pos_r, 1)

            take_dve = {"q": lambda c: rest_part(0, c, tr_flat, True), "k": lambda c: rest_part(1, c, tr_flat, True),
                        "o": normalise, "y": gate_y, "lg": choose, "px": place}

            def gates():
                dve.wait_ge(row_r, 4)
                for row in (ga_row, gb_row):
                    r = row.rearrange("p b e -> p (b e)")
                    link(dve.tensor_scalar(gsign[:], r, 0.0, 2.0, ALU.is_ge, ALU.mult))
                    link(dve.tensor_scalar(gsign[:], gsign[:], 1.0, -1.0, ALU.mult, ALU.add))
                    link(dve.tensor_tensor(gabs[:], gsign[:], r, ALU.mult))
                    link(dve.tensor_scalar(gabs[:], gabs[:], 0.25, None, ALU.max))
                    link(dve.tensor_tensor(r, gsign[:], gabs[:], ALU.mult))
                r = cb_row.rearrange("p b e -> p (b e)")
                link(dve.tensor_scalar(r, r, 1.0, 1.0, ALU.mult, ALU.add))
                dve.sem_inc(gate_r, 1)

            stats_1(1)
            gates()
            for G in range(-2, GROUPS):
                b, g = G // GB, G % GB
                for s in range(UNITS):
                    todo = [(kind, n) for kind, n in extras(G, s) if kind in take_dve]
                    if s % 2 == 0:
                        for kind, n in todo:
                            take_dve[kind](n)
                    if G + 2 < GROUPS:
                        max_unit(G + 2, s)
                    if s % 2:
                        for kind, n in todo:
                            take_dve[kind](n)
                    if s == 1 and G == -1:
                        empty_table()
                    if s == 1 and g == 0 and G >= 0 and b + 2 < B:
                        stats_1(b + 2)
                    if s == 3 and g == 1 and b >= 1:
                        stats_2(b - 1)
                    if s == 4 and g == 2 and b >= 1:
                        weights(b - 1)
                if G + 2 < GROUPS:
                    max_split(G + 2)
            normalise(GROUPS - 1)
            gate_y(B - 1)
            stats_2(B - 1)
            choose(B - 1)
            weights(B - 1)
            place(B - 1)

            link(dve.tensor_tensor(cnt[:], run[:, TT, :], base_e[:], ALU.subtract))
            link(dve.tensor_scalar(cntu[:], cnt[:], float(P - 1), None, ALU.add))
            link(dve.tensor_scalar(cntu[:], cntu[:], 7, None, ALU.logical_shift_right))
            link(dve.tensor_copy(nblk[:], cntu[:]))
            link(dve.tensor_tensor_scan(cum[:], ones_e[:], nblk[:], 0.0, ALU.mult, ALU.add))
            link(dve.tensor_scalar(skip[:], nblk[:], -1.0, float(REGION), ALU.mult, ALU.add))
            link(dve.tensor_scalar(passed[:], cum[:], part_i[:], None, ALU.is_le))
            link(dve.tensor_tensor(passed[:], passed[:], skip[:], ALU.mult))
            link(dve.tensor_reduce(startf[:], passed[:], AX_X, ALU.add))
            link(dve.tensor_tensor(startf[:], startf[:], part_i[:], ALU.add))
            dve.tensor_copy(startu[:], startf[:]).then_inc(start_r, 1)
            shape = (P, BLOCKS, NX)
            link(dve.tensor_tensor(over[:], iota_b[:].rearrange("p (i o) -> p i o", o=1).broadcast_to(shape),
                                   cum[:].rearrange("p (o e) -> p o e", o=1).broadcast_to(shape), ALU.is_ge))
            link(dve.tensor_reduce(eidf[:], over[:], AX_X, ALU.add))
            dve.tensor_scalar(eid[:], eidf[:], float(NX - 1), None, ALU.min).then_inc(eid_r, 1)
            dve.wait_ge(tb_ps, 1)
            dve.tensor_copy(wslot[:], tr_flat[:, P:P + BLOCKS]).then_inc(dchain, 1)
            chain[0] += 1
            link(dve.tensor_copy(dest[:], tr_flat[:, 0:BLOCKS]))
            dve.tensor_scalar(srcs[:], dest[:], TOK - 1, None, ALU.bitwise_and).then_inc(dest_r, 1)

            def keep_x(i):
                dve.wait_ge(xbT_ps, i + 1)
                if i >= 2:
                    dve.wait_ge(h_ps, i - 1)
                dve.tensor_copy(xbT[i % 2][:], xp[i % 2]).then_inc(xbT_r, 1)

            def pick_w1(i):
                if i % LOADS == 0:
                    load_experts(i)
                if i >= WR:
                    dve.wait_ge(g_r, i - WR + 1)
                dve.tensor_copy(w1_blk[i % WR], w1_all[:, bass.ds(expert[i] * WB, WB)]).then_inc(w1_r, 1)

            def load_experts(i):
                n = min(LOADS, BLOCKS - i)
                _, values = nc.values_load_multi_w_load_instructions(
                    eid[0:1, i:i + n], engines=[mybir.EngineType.DVE], min_val=0, max_val=NX - 1,
                    skip_runtime_bounds_check_because="a block's expert was clamped to 0 .. NX - 1")
                for k in range(n):
                    expert[i + k] = values[k]

            def add_b2(i):
                dve.wait_ge(yb_ps, i + 1)
                if i >= 2:
                    dve.wait_ge(yb_r, i - 1)
                dve.tensor_tensor(yc[i % 2][:], sc[i % 2][:, 0:E], b2_row[:, bass.ds(expert.pop(i) * E, E)],
                                  ALU.add).then_inc(yc_r, 1)

            expert = {}
            dve.wait_ge(eid_r, 1)
            dve.wait_ge(we_in, 32 * NX + 16)
            pick_w1(0)
            pick_w1(1)
            keep_x(0)
            for i in range(BLOCKS + 1):
                if i + 1 < BLOCKS:
                    keep_x(i + 1)
                if i + 2 < BLOCKS:
                    pick_w1(i + 2)
                if i >= 1:
                    add_b2(i - 1)
            for b in range(B):
                xd = x_all[:, b * TT:(b + 1) * TT, :]
                dve.wait_ge(ysum_r, b + 1)
                link(dve.tensor_tensor(y_of(b, 1), y_of(b, 0), gb_row[:, b:b + 1, :].broadcast_to((P, TT, E)), ALU.mult))
                dve.tensor_tensor(xd, xd, y_of(b, 1), ALU.add).then_inc(fin_r, 1)

        @block.tensor
        def _(pe):
            def take(kind, n):
                uses = order[:turn[(kind, n)]]
                last = {}
                for k, m in uses:
                    last[k] = m
                for k, m in last.items():
                    sem_, per = READ[k]
                    if turn[(k, m)] >= turn[(kind, n)] - 2:
                        pe.wait_ge(sem_, m + 1)

            READ = {"xnT": (hT_r, 1), "q": (rest_r[0], 1), "k": (rest_r[1], 1), "v": (v_r, 1), "m": (mrow_r, 1),
                    "o": (attn_r, 1), "aT": (aT_r, 1), "y": (ytmp_r, 1), "h2T": (h2T_r, 1), "lg": (lg_r, 1),
                    "px": (px_r, 1), "tb": (dest_r, 1)}

            pe.wait_ge(silu_r, 1)
            for m in range(2):
                last = pe.matmul(pv[:, B * m:B * (m + 1)], wmb[:, E * m:E * (m + 1)], silu[:], start=True, stop=True)
            last.then_inc(mod_ps, 1)
            pe.wait_ge(consts, 4)

            def turn_x(c):
                take("xnT", c)
                pe.wait_ge(xn_r, c + 1)
                for t in range(TT):
                    last = pe.transpose(tr[:, t, :], xn[:, t, :], ident[:])
                last.then_inc(xnT_ps, 1)

            def project(n, c, dst):
                pe.wait_ge(hT_r, c + 1)
                pe.matmul(dst, (wqpb, wkpb)[n][:], hT[:], start=True, stop=True).then_inc(qk_ps[n], 1)

            def project_v(c, dst):
                for t in range(TT):
                    last = pe.matmul(dst[:, P * t:P * (t + 1)], hT[:, P * t:P * (t + 1)], wkb[:],
                                     start=True, stop=True)
                last.then_inc(v_ps, 1)

            turn_x(0)
            pe.wait_ge(wb_in, 48)
            for n in range(2):
                project(n, 0, mx[n][:, 0, :])
            project_v(0, sc[0][:])
            pe.wait_ge(mod_r, 1)
            for m, bank in zip((2, 5, 4, 3), (mx[0][:, 1, :], mx[1][:, 1, :], sc[1][:], pv[:])):
                for b in range(B):
                    last = pe.matmul(bank[:, E * b:E * (b + 1)], silu_w[:, b, :], wmb[:, E * m:E * (m + 1)],
                                     start=True, stop=True)
            last.then_inc(row_ps, 1)

            def maxima(G, n):
                b, g = G // GB, G % GB
                u, c = n // 2, n % 2
                if n == 0:
                    pe.wait_ge(ld[g], LDG * (b + 1))
                if c == 0 and UNITS * G + u >= 2:
                    pe.wait_ge(mx_used, UNITS * G + u - 1)
                j, qt = n // TT, n % TT
                ins = pe.matmul(mx[u % 2][:, c, :], qs[g][0:MROW, j, P * qt:P * (qt + 1)],
                                ks[g][0:MROW, j, :], start=True, stop=True)
                if c == 1:
                    ins.then_inc(mx_ready, 1)

            def score(G, n):
                b, g = G // GB, G % GB
                kt, j = n // HG, n % HG
                if n == 0:
                    pe.wait_ge(ldm[g], 16 * (b + 1))
                if NS * G + n >= 2:
                    pe.wait_ge(p_ready, NS * G + n - 1)
                pe.matmul(sc[n % 2][:], ks[g][0:KEXP, j, P * kt:P * (kt + 1)], qs[g][0:KEXP, j, :],
                          start=True, stop=True).then_inc(sc_ready, 1)

            def weigh(G, kt):
                pe.wait_ge(p_ready, NS * G + HG * (kt + 1))
                if kt == 0:
                    pe.wait_ge(vcur_r, G + 1)
                    if G:
                        pe.wait_ge(o_r, G)
                for j in range(HG):
                    last = pe.matmul(pv[32 * j:32 * (j + 1), :], vcur[G % 2][:, kt, j, :], probs[:, kt, j, :],
                                     start=kt == 0, stop=kt == TT - 1, skip_group_check=True)
                last.then_inc(pv_done, 1)

            def turn_max(G):
                take("m", G)
                pe.wait_ge(mneg_r, G + 1)
                pe.transpose(tr_m[0:PARTS * NS, 0:P], mneg[G % 2][:].rearrange("p i n -> p (i n)"),
                             identb[:]).then_inc(mT_ps, 1)

            def turn_out(G):
                take("o", G)
                pe.wait_ge(o_r, G + 1)
                for t in range(TT):
                    last = pe.transpose(tr[:, t, :], o_sb[:, P * t:P * (t + 1)], ident[:])
                last.then_inc(oT_ps, 1)

            def turn_attn(d):
                take("aT", d)
                pe.wait_ge(attn_r, GB * (d + 1))
                for t in range(TT):
                    last = pe.transpose(tr[:, t, :], attn[:, d * TT + t, :], ident[:])
                last.then_inc(aT_ps, 1)

            def out_proj(d):
                take("y", d)
                pe.wait_ge(aT_r, d + 1)
                pe.wait_ge(wc_in, 48)
                for t in range(TT):
                    last = pe.matmul(tr[:, t, :], aT[:, P * t:P * (t + 1)], wob[:], start=True, stop=True)
                last.then_inc(y_ps, 1)

            def turn_h2(d):
                take("h2T", d)
                pe.wait_ge(h2_r, d + 1)
                for t in range(TT):
                    last = pe.transpose(tr[:, t, :], h2[:, t, :], ident[:])
                last.then_inc(h2T_ps, 1)

            def route(d):
                take("lg", d)
                pe.wait_ge(h2T_r, d + 1)
                for t in range(TT):
                    last = pe.matmul(tr_flat[:, NX * t:NX * (t + 1)], h2T[:, P * t:P * (t + 1)], rwb[:],
                                     start=True, stop=True)
                last.then_inc(lg_ps, 1)

            def rank(d):
                take("px", d)
                pe.wait_ge(hot_r, d + 1)
                pe.wait_ge(consts, 6)
                h = hots[:].rearrange("p t e -> p (t e)")
                pe.matmul(tr_flat[:, 0:TT * NX], before[:], h, start=True, stop=True)
                pe.matmul(tr_flat[:, TT * NX:2 * TT * NX], onesb[:], h, start=True, stop=True).then_inc(px_ps, 1)

            work = {"xnT": turn_x, "q": lambda c: (take("q", c), project(0, c, tr_flat)),
                    "k": lambda c: (take("k", c), project(1, c, tr_flat)),
                    "v": lambda c: (take("v", c), project_v(c, tr_flat)),
                    "m": turn_max, "o": turn_out,
                    "aT": turn_attn, "y": out_proj, "h2T": turn_h2, "lg": route, "px": rank}

            pe.wait_ge(row_r, 4)
            pe.wait_ge(v_r, 1)
            for n in range(2):
                pe.wait_ge(rest_r[n], 1)
            for G in range(-2, GROUPS):
                for p in range(TT):
                    if G >= 0:
                        score(G, 4 * p)
                        score(G, 4 * p + 1)
                        if p == 0 and G >= 1:
                            weigh(G - 1, TT - 1)
                        if p >= 1:
                            weigh(G, p - 1)
                    for kind, n in extras(G, 2 * p):
                        work[kind](n)
                    if G >= 0:
                        score(G, 4 * p + 2)
                    if G + 2 < GROUPS:
                        maxima(G + 2, 4 * p)
                    if G >= 0:
                        score(G, 4 * p + 3)
                    if G + 2 < GROUPS:
                        for n in range(1, 4):
                            maxima(G + 2, 4 * p + n)
                    for kind, n in extras(G, 2 * p + 1):
                        work[kind](n)
            weigh(GROUPS - 1, TT - 1)
            turn_out(GROUPS - 1)
            for kind in ("aT", "y", "h2T", "lg", "px"):
                work[kind](B - 1)
            take("tb", 0)
            pe.wait_ge(tabT_in, 16)
            for c in range(2):
                last = pe.transpose(tr_flat[:, P * c:P * c + BLOCKS], tabT[:, :, c], ident[0:BLOCKS, 0:BLOCKS])
            last.then_inc(tb_ps, 1)

            pe.wait_ge(eid_r, 1)
            pe.wait_ge(we_in, 32 * NX + 16)
            pe.wait_ge(dest_r, 1)

            def turn_block(i):
                pe.wait_ge(xb_in[i % XR], 16 * (i // XR + 1))
                if i >= 2:
                    pe.wait_ge(xbT_r, i - 1)
                pe.transpose(xp[i % 2], xb[i % XR][:], ident[:]).then_inc(xbT_ps, 1)

            def experts_from(i):
                n = min(LOADS, BLOCKS - i)
                _, values = nc.values_load_multi_w_load_instructions(
                    eid[0:1, i:i + n], engines=[mybir.EngineType.PE], min_val=0, max_val=NX - 1,
                    skip_runtime_bounds_check_because="DVE clamps a block's expert to 0 .. NX - 1")
                for k in range(n):
                    expert[i + k] = values[k]

            def expand(i):
                pe.wait_ge(xbT_r, i + 1)
                pe.wait_ge(w1_r, i + 1)
                if i >= 2:
                    pe.wait_ge(g_r, i - 1)
                for f in range(FC):
                    last = pe.matmul(mx[0][:, i % 2, P * f:P * (f + 1)], w1_blk[i % WR][:, P * f:P * (f + 1)],
                                     xbT[i % 2][:], start=True, stop=True)
                last.then_inc(h_ps, 1)

            def contract(i, e):
                pe.wait_ge(g_r, i + 1)
                if i >= 2:
                    pe.wait_ge(yc_r, i - 1)
                y = sc[i % 2][:, 0:E]
                for f in range(FC):
                    last = pe.matmul(y, g_sb[i % 2][:, P * f:P * (f + 1)], w2_all[:, bass.ds(e * (FC * E) + f * E, E)],
                                     start=f == 0, stop=f == FC - 1)
                last.then_inc(yb_ps, 1)

            expert = {}
            turn_block(0)
            for i in range(BLOCKS + 1):
                if i < BLOCKS:
                    if i % LOADS == 0:
                        experts_from(i)
                    expand(i)
                if i + 1 < BLOCKS:
                    turn_block(i + 1)
                if i >= 1:
                    contract(i - 1, expert.pop(i - 1))


_ARGS = ["x", "cT", "wk", "wqp", "wkp", "wo", "bo", "router_wT", "w1b", "w2T", "b2", "wmod"]


def kernel(L0_attn_x, L0_attn_Wk, L0_attn_Wq, L0_attn_Wo, L0_attn_bo, L0_ffn_router_w, L0_ffn_w1,
           L0_ffn_b1, L0_ffn_w2, L0_ffn_b2, L0_c, L0_wmod):
    import numpy as np
    import concourse.bacc as bacc
    from concourse.bass_utils import run_bass_kernel_spmd

    n_x, ff, e = L0_ffn_w1.shape
    w1 = np.asarray(L0_ffn_w1)
    w2 = np.asarray(L0_ffn_w2)

    def by_group(w):
        return np.asarray(w).reshape(e, HEADS // HG, HG, e // HEADS).transpose(0, 1, 3, 2).reshape(e, e)

    laid = {
        "x": np.asarray(L0_attn_x),
        "cT": np.asarray(L0_c).T,
        "wk": np.asarray(L0_attn_Wk), "wo": np.asarray(L0_attn_Wo),
        "wqp": by_group(L0_attn_Wq), "wkp": by_group(L0_attn_Wk),
        "bo": np.asarray(L0_attn_bo).reshape(1, e),
        "router_wT": np.asarray(L0_ffn_router_w).T,
        "w1b": np.concatenate([w1.transpose(2, 0, 1),
                               np.asarray(L0_ffn_b1).reshape(n_x, ff // 128, 128).transpose(2, 0, 1)], 2)
                 .reshape(e, -1),
        "w2T": w2.transpose(0, 2, 1).reshape(n_x, ff // 128, 128, e).transpose(2, 0, 1, 3)
                 .reshape(128, n_x * ff // 128 * e),
        "b2": np.asarray(L0_ffn_b2).reshape(1, n_x * e),
        "wmod": np.asarray(L0_wmod),
    }
    laid = {k: np.ascontiguousarray(v) for k, v in laid.items()}
    nc = bacc.Bacc("TRN2", target_bir_lowering=False, num_devices=1)
    aps = [nc.dram_tensor(f"in_{k}", laid[k].shape, mybir.dt.from_np(laid[k].dtype), kind="ExternalInput").ap()
           for k in _ARGS]
    out = nc.dram_tensor("out_x", laid["x"].shape, F32, kind="ExternalOutput").ap()
    build(nc, *aps, out)
    r = run_bass_kernel_spmd(nc, [{f"in_{k}": laid[k] for k in _ARGS}], core_ids=[0])
    return r.results[0]["out_x"]
```

```python
from contextlib import ExitStack

import concourse.bass as bass
from concourse import mybir
from concourse.alu_op_type import AluOpType as ALU

F32 = mybir.dt.float32
BF16 = mybir.dt.bfloat16
U32 = mybir.dt.uint32
ACT = mybir.ActivationFunctionType
AX_X = mybir.AxisListType.X

P = 128
HEADS = 16
HG = 4
EPS = 1e-5
PARTS = 3
RING = 4
ONES_PAIR = 1 + 0x3F80 / 2.0 ** 23


def build(nc, x, cT, wk, wqp, wkp, wo, bo, router_wT, w1b, w2T, b2, wmod, out):
    B, T, E = x.shape
    S = E // HEADS
    TT = T // P
    NT = B * TT
    GB = HEADS // HG
    NX = router_wT.shape[1]
    FC = w2T.shape[1] // (NX * E)
    FF = FC * P
    WB = FF + FC
    TOK = B * T
    PROD = PARTS * PARTS * S
    MROW = 96
    KEXP = MROW + PARTS
    EXP_SCALE = float(E) ** -0.5
    GROUPS = B * GB
    UNITS = 2 * HG
    NS = HG * TT
    LDG = 16 * (1 + PARTS)
    BLOCKS = (2 * TOK - NX) // P + NX
    REGION = TOK // P + 1
    SLOTS = NX * REGION * P
    ROW = E + 2
    FULL = -(-(2 * (TOK - T) - NX * (P - 1)) // P)
    PART = [range(0, FULL), range(FULL, BLOCKS)]
    LIST_AT = (9, 10, 11)
    PADS_AT = 15
    ENTER_AT = 7
    POOL_BATCH = 1
    LOADS = 8
    PAD = 2 * TOK
    assert E == P and T == 512 and GB == RING and PROD <= MROW and TOK & (TOK - 1) == 0

    with ExitStack() as ctx:
        def sb(name, shape, dt=F32):
            return ctx.enter_context(nc.sbuf_tensor(name, shape, dt))

        def psum(name, shape, dt=F32):
            return ctx.enter_context(nc.psum_tensor(name, shape, dt))

        def sem(name):
            return ctx.enter_context(nc.semaphore(name))

        q_scr = nc.dram_tensor("q_scr", (B, GB, PARTS, S, HG * T), BF16).ap()
        k_scr = nc.dram_tensor("k_scr", (B, GB, PARTS, S, HG * T), BF16).ap()
        slots_scr = nc.dram_tensor("slots_scr", (SLOTS + P, ROW), F32).ap()
        y_scr = nc.dram_tensor("y_scr", (2 * TOK, E), F32).ap()

        x_all = sb("x_all", [P, NT, E])
        v_all = sb("v_all", [P, NT, E])
        attn = sb("attn", [P, NT, E])
        w1_all = sb("w1_all", [P, NX * WB])
        w2_all = sb("w2_all", [P, NX * FC * E])
        wkb = sb("wkb", [P, E])
        wqpb = sb("wqpb", [P, E])
        wkpb = sb("wkpb", [P, E])
        wob = sb("wob", [P, E])
        rwb = sb("rwb", [P, NX])
        wmb = sb("wmb", [P, 6 * E])
        bob = sb("bob", [P, E])
        ctb = sb("ctb", [P, B])
        sig = sb("sig", [P, B])
        silu = sb("silu", [P, B])
        silu_w = sb("silu_w", [P, B, P])
        modc = sb("modc", [P, 2, B])
        mod_row = sb("mod_row", [P, 4, B, E])
        ga_row, gb_row, cb_row, sb_row = (mod_row[:, n] for n in range(4))
        gsign = sb("gsign", [P, B * E])
        gabs = sb("gabs", [P, B * E])
        gabo = sb("gabo", [P, E])
        ident = sb("ident", [P, P])
        identb = sb("identb", [P, P], BF16)
        before = sb("before", [P, P], BF16)
        onesb = sb("onesb", [P, P], BF16)
        stats = sb("stats", [P, TT, 6])
        mv = sb("mv", [P, TT, 2])
        vareps = sb("vareps", [P, TT])
        rstd = sb("rstd", [P, TT])
        mhalf = sb("mhalf", [P, TT])
        xn = sb("xn", [P, TT, E])
        hT = sb("hT", [P, T])
        parts = [sb(f"parts_{n}", [P, PARTS, T], BF16) for n in "qk"]
        rest = [sb(f"rest_{n}", [P, T]) for n in "qk"]
        qs = [sb(f"qs{r}", [P, HG, T], BF16) for r in range(RING)]
        ks = [sb(f"ks{r}", [P, HG, T], BF16) for r in range(RING)]
        mcol = sb("mcol", [P, NS])
        mres = sb("mres", [P, NS])
        mneg = [sb(f"mneg{r}", [P, PARTS, NS], BF16) for r in range(2)]
        mrow = [sb(f"mrow{r}", [PARTS * NS, P], BF16) for r in range(2)]
        vcur = [sb(f"vcur{r}", [P, TT, HG, 32]) for r in range(2)]
        probs = sb("probs", [P, TT, HG, T])
        o_sb = sb("o_sb", [P, T])
        rden = sb("rden", [P, TT, HG])
        aT = sb("aT", [P, T])
        ytmp = sb("ytmp", [P, TT, E])
        xn2 = sb("xn2", [P, TT, E])
        h2c = sb("h2c", [P, 2, TT, ROW])
        h2 = h2c[:, 0, :, 0:E]
        h2T = sb("h2T", [P, T])
        top = sb("top", [P, TT, 8])
        topi = sb("topi", [P, TT, 8], U32)
        topf = sb("topf", [P, 2, TT])
        wexp = sb("wexp", [P, TT])
        wden = sb("wden", [P, TT])
        logits = sb("logits", [P, TT, NX])
        iota_e = sb("iota_e", [P, NX])
        hot = sb("hot", [P, 2, TT, NX])
        hots = sb("hots", [P, TT, NX], BF16)
        run = sb("run", [P, TT + 1, NX])
        ranks = sb("ranks", [P, 2 * TT * NX])
        slots = sb("slots", [P, TT, NX])
        hslots = sb("hslots", [P, 2 * TT, NX])
        posf = sb("posf", [P, 2 * TT])
        pos = [sb(f"pos{r}", [P, 2 * TT], U32) for r in range(2)]
        tok_id = sb("tok_id", [P, 2, NT])
        pads = sb("pads", [P, ROW])
        end_u = sb("end_u", [P, NX], U32)
        base_e = sb("base_e", [P, NX])
        cnt = sb("cnt", [P, NX])
        cntu = sb("cntu", [P, NX], U32)
        nblk = sb("nblk", [P, NX])
        ones_e = sb("ones_e", [P, NX])
        cum = sb("cum", [P, NX])
        skip = sb("skip", [P, NX])
        startf = sb("startf", [P, BLOCKS])
        startu = sb("startu", [P, BLOCKS], U32)
        capped = sb("capped", [P, NX + 1])
        taken = sb("taken", [P, NX + 1])
        iota_b = sb("iota_b", [P, BLOCKS])
        over = sb("over", [P, BLOCKS, NX])
        eidf = sb("eidf", [P, BLOCKS])
        eid = sb("eid", [P, BLOCKS], U32)
        dest = sb("dest", [P, BLOCKS], U32)
        b2_row = sb("b2_row", [P, NX * E])
        XR = 6
        WR = 4
        xb = [sb(f"xb{r}", [P, ROW]) for r in range(XR)]
        xbT = [sb(f"xbT{r}", [P, P]) for r in range(2)]
        w1_blk = [qs[r][:].rearrange("p h t -> p (h t)").bitcast(F32)[:, 0:WB] for r in range(WR)]
        g_sb = [ks[r][:].rearrange("p h t -> p (h t)").bitcast(F32)[:, 0:FF] for r in range(2)]
        yc = [sb(f"yc{r}", [P, E]) for r in range(2)]
        yb = [sb(f"yb{r}", [P, E]) for r in range(XR)]
        y_room = (probs[:].rearrange("p a h t -> p (a h t)")[:, 0:2 * NT * E]
                  .rearrange("p (b t n e) -> p b t n e", b=B, t=TT, n=2, e=E))

        def y_of(b, n):
            return y_room[:, b, :, n, :]

        def gated_sum(engine, link, b):
            xd = x_all[:, b * TT:(b + 1) * TT, :]
            link(engine.tensor_tensor(y_of(b, 0), y_of(b, 0), gb_row[:, b:b + 1, :].broadcast_to((P, TT, E)), ALU.mult))
            return engine.tensor_tensor(xd, xd, y_of(b, 0), ALU.add)

        mx = [psum(f"mx{r}", [P, 2, T]) for r in range(2)]
        sc = [psum(f"sc{r}", [P, T]) for r in range(2)]
        pv = psum("pv", [P, T])
        tr = psum("tr", [P, TT, P])
        tr_flat = tr[:].rearrange("p t e -> p (t e)")
        tr_m = tr[:, 0, :].bitcast(BF16)
        xp = [mx[1][:, r, 0:P] for r in range(2)]

        FREE = NS * (GROUPS - 2) + HG

        def score_bank(n):
            last = n - FREE
            if last < 0:
                return sc[n % 2][:], 2
            banks = [sc[r][:] for r in range(2)] + [mx[r][:, c, :] for r in range(2) for c in range(2)]
            return banks[last % 6], 2 if last < 2 else 6

        x_in = [sem(f"x_in{b}") for b in range(B)]
        c_in = sem("c_in"); wa_in = sem("wa_in"); wb_in = sem("wb_in"); wc_in = sem("wc_in"); we_in = sem("we_in")
        pads_r = [sem(f"pads_r{r}") for r in range(RING)]; vpad_r = sem("vpad_r")
        pool_k = sem("pool_k"); consts = sem("consts"); dchain = sem("dchain"); pchain = sem("pchain")
        sig_r = sem("sig_r"); silu_r = sem("silu_r"); mod_ps = sem("mod_ps"); mod_r = sem("mod_r")
        row_ps = sem("row_ps"); row_r = sem("row_r"); gate_r = sem("gate_r")
        stat_r = sem("stat_r"); rstd0_r = sem("rstd0_r"); xn_r = sem("xn_r"); xnT_ps = sem("xnT_ps")
        hT_r = sem("hT_r"); q_ps = sem("q_ps"); k_ps = sem("k_ps"); v_ps = sem("v_ps")
        qk_ps = [q_ps, k_ps]
        part1 = [sem(f"part1_{n}") for n in "qk"]
        rest_r = [sem(f"rest_{n}") for n in "qk"]
        part2 = [sem(f"part2_{n}") for n in "qk"]
        part3 = [sem(f"part3_{n}") for n in "qk"]
        scr_w = [sem(f"scr_w_{n}") for n in "qk"]
        v_r = sem("v_r"); lg_r = sem("lg_r"); px_r = sem("px_r"); tabz = sem("tabz")
        ld = [sem(f"ld{r}") for r in range(RING)]
        ldm = [sem(f"ldm{r}") for r in range(RING)]
        mx_ready = sem("mx_ready"); mx_used = sem("mx_used"); mneg_r = sem("mneg_r")
        mT_ps = sem("mT_ps"); mrow_r = sem("mrow_r")
        sc_ready = sem("sc_ready"); p_ready = sem("p_ready"); vcur_r = sem("vcur_r")
        pv_done = sem("pv_done"); o_r = sem("o_r"); oT_ps = sem("oT_ps"); attn_r = sem("attn_r")
        aT_ps = sem("aT_ps"); aT_r = sem("aT_r"); y_ps = sem("y_ps"); ytmp_r = sem("ytmp_r")
        x2_r = sem("x2_r"); stat2_r = sem("stat2_r"); h2_r = sem("h2_r"); h2T_ps = sem("h2T_ps")
        h2T_r = sem("h2T_r"); lg_ps = sem("lg_ps"); top_r = sem("top_r"); wexp_r = sem("wexp_r")
        hot_r = sem("hot_r"); px_ps = sem("px_ps"); pos_r = sem("pos_r")
        pad_w = sem("pad_w"); h2b_r = sem("h2b_r"); end_r = sem("end_r"); ent_w = [sem(f"ent_w{r}") for r in range(2)]
        start_r = sem("start_r"); eid_r = sem("eid_r"); bias_r = sem("bias_r"); rstd_r = sem("rstd_r")
        dest_r = sem("dest_r")
        xb_in = [sem(f"xb_in{r}") for r in range(XR)]
        xbT_ps = sem("xbT_ps"); xbT_r = sem("xbT_r"); h_ps = sem("h_ps"); w1_r = sem("w1_r"); g_r = sem("g_r")
        yb_ps = sem("yb_ps"); yc_r = sem("yc_r"); yb_r = sem("yb_r")
        y_w = [sem(f"y_w{r}") for r in range(XR)]
        y_in = [sem(f"y_in{b}") for b in range(B)]
        fin_r = [sem(f"fin_r{b}") for b in range(B)]; out_w = sem("out_w")

        def extras(G, s):
            b, g = G // GB, G % GB
            todo = []
            if s == 2 and 0 <= G + 1 < GROUPS:
                todo.append(("m", G + 1))
            if s == 4 and G >= 1:
                todo.append(("o", G - 1))
            c = b + 2 if g == 3 else b + 1
            if G >= -1 and 1 <= c < B:
                todo += [(kind, c) for kind in {(3, 0): ("xnT",), (3, 3): ("q",), (3, 5): ("k",),
                                                (0, 1): ("v",)}.get((g, s), ())]
            if b >= 1:
                todo += [(kind, b - 1) for kind in {(0, 7): ("aT",), (1, 0): ("y",), (2, 0): ("h2T",),
                                                    (2, 1): ("lg",), (2, 3): ("px",)}.get((g, s), ())]
            return todo

        uses = [("xnT", 0)]
        for G in range(-2, GROUPS):
            for s in range(UNITS):
                uses += extras(G, s)
        LAST = {0: "aT", 1: "y", 5: "h2T", 6: "lg", 7: "px"}
        uses += [("o", GROUPS - 1)] + [(LAST[i], B - 1) for i in sorted(LAST)]
        turn = {use: n for n, use in enumerate(uses)}

        block = ctx.enter_context(nc.Block())

        @block.sync
        def _(sp):
            sp.dma_start(x_all[:, 0:TT, :], x[0].rearrange("(t p) e -> p t e", p=P)).then_inc(x_in[0], 16)
            sp.dma_start(ctb[:], cT).then_inc(c_in, 16)
            sp.dma_start(wmb[:], wmod).then_inc(wa_in, 16)
            for dst, src in ((wqpb[:], wqp), (wkpb[:], wkp), (wkb[:], wk)):
                sp.dma_start(dst, src).then_inc(wb_in, 16)
            for b in range(1, B):
                sp.dma_start(x_all[:, b * TT:(b + 1) * TT, :],
                             x[b].rearrange("(t p) e -> p t e", p=P)).then_inc(x_in[b], 16)
            for dst, src in ((wob[:], wo), (rwb[:], router_wT), (bob[:], bo.broadcast_to((P, E)))):
                sp.dma_start(dst, src).then_inc(wc_in, 16)

            def store_parts(n, c):
                sp.wait_ge(part3[n], c + 1)
                scr = (q_scr, k_scr)[n]
                for i in range(PARTS):
                    sp.dma_start(scr[c, :, i].rearrange("g s (h t) -> g (s h) t", t=T),
                                 parts[n][:, i, :]).then_inc(scr_w[n], 16)

            def load(G):
                b, g = G // GB, G % GB
                for n in range(2):
                    sp.wait_ge(scr_w[n], 16 * PARTS * (b + 1))
                if G >= RING:
                    sp.wait_ge(sc_ready, NS * (G - RING + 1))
                ksrc = k_scr[b, g].rearrange("(o j) s n -> o (j s) n", o=1)
                sp.dma_start(ks[g][0:PROD].rearrange("p h t -> p (h t)"),
                             ksrc.broadcast_to((PARTS, PARTS * S, HG * T))).then_inc(ld[g], 16)
                for i in range(PARTS):
                    qsrc = q_scr[b, g, i:i + 1].broadcast_to((PARTS, S, HG * T))
                    sp.dma_start(qs[g][PARTS * S * i:PARTS * S * (i + 1)].rearrange("p h t -> p (h t)"),
                                 qsrc).then_inc(ld[g], 16)

            def load_max(G):
                g = G % GB
                sp.wait_ge(mrow_r, G + 1)
                sp.dma_start(qs[g][MROW:KEXP].rearrange("i h (q t) -> i (h q) t", t=P),
                             mrow[G % 2][:]).then_inc(ldm[g], 16)

            def load_rows(r):
                for h in range(2):
                    sp.wait_ge(ent_w[h], 16 * 2 * TT * len(range(h, B - 1 + r, 2)))
                sp.wait_ge(start_r, r + 1)
                end = PART[r].stop
                for a in range(PART[r].start, end, LOADS):
                    n = min(LOADS, end - a)
                    _, values = nc.values_load_multi_w_load_instructions(
                        startu[0:1, a:a + n], engines=[mybir.EngineType.SP], min_val=0, max_val=SLOTS,
                        skip_runtime_bounds_check_because="DVE clamps a block's first slot to 0 .. SLOTS")
                    for i in range(a, a + n):
                        if i == PADS_AT:
                            store_pads()
                        if i >= XR:
                            sp.wait_ge(yb_r, i - XR + 1)
                        sp.dma_start(xb[i % XR][:], slots_scr[bass.ds(values[i - a], P), :]).then_inc(xb_in[i % XR], 16)

            def store_pads():
                sp.wait_ge(end_r, 1)
                _, values = nc.values_load_multi_w_load_instructions(
                    end_u[0:1, :], engines=[mybir.EngineType.SP], min_val=0, max_val=SLOTS - P,
                    skip_runtime_bounds_check_because="an expert has at most TOK of its region's TOK + P slots")
                for e in range(NX):
                    sp.dma_start(slots_scr[bass.ds(values[e], P), :], pads[:]).then_inc(pad_w, 16)

            for i, ready in enumerate((part1, part2, part3)):
                for n in range(2):
                    sp.wait_ge(ready[n], 1)
                    sp.dma_start((q_scr, k_scr)[n][0, :, i].rearrange("g s (h t) -> g (s h) t", t=T),
                                 parts[n][:, i, :]).then_inc(scr_w[n], 16)
            for G in range(RING):
                sp.wait_ge(pads_r[G], 1)
                load(G)
            for G in range(-1, GROUPS):
                g = G % GB
                if 1 <= G and G + 3 < GROUPS:
                    load(G + 3)
                if G + 1 < GROUPS:
                    load_max(G + 1)
                if g == 3 and (G + 5) // GB < B:
                    store_parts(0, (G + 5) // GB)
                if g == 0 and (G + 4) // GB < B:
                    store_parts(1, (G + 4) // GB)
                if G == 0:
                    sp.wait_ge(tabz, 1)
                    sp.dma_start(slots_scr[SLOTS:SLOTS + P, :], pads[:]).then_inc(pad_w, 16)
                if 2 <= G < 2 + NX:
                    e = G - 2
                    sp.dma_start(w1_all[:, WB * e:WB * (e + 1)], w1b[:, WB * e:WB * (e + 1)]).then_inc(we_in, 16)
                    sp.dma_start(w2_all[:, FC * E * e:FC * E * (e + 1)],
                                 w2T[:, FC * E * e:FC * E * (e + 1)]).then_inc(we_in, 16)
                if G == 2 + NX:
                    sp.dma_start(b2_row[:], b2.broadcast_to((P, NX * E))).then_inc(we_in, 16)
            load_rows(0)
            sp.wait_ge(pad_w, 16 * (NX + 1))
            load_rows(1)
            for r in range(XR):
                sp.wait_ge(y_w[r], 16 * len(range(r, BLOCKS, XR)))
            for b in range(B):
                sp.dma_start(y_room[:, b].rearrange("p t n e -> p (t n) e"),
                             y_scr[2 * T * b:2 * T * (b + 1), :].rearrange("(r p) e -> p r e", p=P)).then_inc(y_in[b], 16)
            for b in sorted(range(B), key=lambda b: b + 1.5 * (b == POOL_BATCH)):
                sp.wait_ge(fin_r[b], 1)
                sp.dma_start(out[b].rearrange("(t p) e -> p t e", p=P),
                             x_all[:, b * TT:(b + 1) * TT, :]).then_inc(out_w, 16)
            sp.wait_ge(out_w, 16 * B)

        @block.gpsimd
        def _(pool):
            chain = [0]

            def link(ins):
                chain[0] += 1
                ins.then_inc(pchain, 1)
                pool.wait_ge(pchain, chain[0])

            pool.memset(mhalf[:], -0.5).then_inc(consts, 1)
            pool.memset(ident[:], 0.0).then_inc(pool_k, 1)
            pool.memset(identb[:], 0.0).then_inc(pool_k, 1)
            pool.memset(onesb[:], 1.0).then_inc(consts, 1)
            pool.memset(before[:], 1.0).then_inc(pool_k, 1)
            pool.wait_ge(pool_k, 3)
            for m in (ident, identb):
                pool.affine_select(out=m[:], in_=m[:], compare_op=ALU.not_equal, fill=1.0, base=0,
                                   pattern=[[-1, P]], channel_multiplier=1).then_inc(consts, 1)

            def layer_norm(src, b, ready, n, dst, done):
                pool.wait_ge(ready, n)
                link(pool.tensor_tensor(rstd[:], vareps[:], mhalf[:], ALU.pow))
                bc = (P, TT, E)
                link(pool.tensor_tensor(dst[:], src[:, b * TT:(b + 1) * TT, :], mv[:, :, 0:1].broadcast_to(bc), ALU.subtract))
                last = pool.tensor_tensor(dst[:], dst[:], rstd[:].rearrange("p (t o) -> p t o", o=1).broadcast_to(bc), ALU.mult)
                if done is None:
                    link(last)
                else:
                    last.then_inc(done, 1)

            def norm1(c):
                if c:
                    pool.wait_ge(xnT_ps, c)
                layer_norm(x_all, c, stat_r, c + 1, xn, xn_r)

            def pad_ring(r):
                link(pool.memset(ks[r][64:96].rearrange("p h t -> p (h t)").bitcast(F32), 0.0))
                link(pool.memset(ks[r][96:128].rearrange("p h t -> p (h t)").bitcast(F32), ONES_PAIR))
                link(pool.memset(qs[r][64:128].rearrange("p h t -> p (h t)").bitcast(F32), 0.0))
                pool.sem_inc(pads_r[r], 1)

            pool.wait_ge(consts, 4)
            pad_ring(2)
            pool.wait_ge(stat_r, 1)
            link(pool.tensor_tensor(rstd[:], vareps[:], mhalf[:], ALU.pow))
            pool.sem_inc(rstd0_r, 1)
            pad_ring(3)
            pool.affine_select(out=before[:], in_=before[:], compare_op=ALU.is_gt, fill=0.0, base=0,
                               pattern=[[1, P]], channel_multiplier=-1).then_inc(consts, 1)
            for r in range(2):
                link(pool.memset(vcur[r][:], 0.0))
                pool.memset(vcur[r][:, :, :, S:S + 1], 1.0).then_inc(vpad_r, 1)
            pool.iota(iota_e[:], pattern=[[1, NX]], base=0, channel_multiplier=0,
                      allow_small_or_imprecise_dtypes=True).then_inc(consts, 1)
            pool.iota(iota_b[:], pattern=[[1, BLOCKS]], base=0, channel_multiplier=0,
                      allow_small_or_imprecise_dtypes=True).then_inc(consts, 1)
            pool.iota(tok_id[:], pattern=[[P, 2], [2 * P, NT]], base=0, channel_multiplier=1,
                      allow_small_or_imprecise_dtypes=True).then_inc(consts, 1)
            pool.iota(base_e[:], pattern=[[REGION * P, NX]], base=0, channel_multiplier=0,
                      allow_small_or_imprecise_dtypes=True).then_inc(consts, 1)
            pool.memset(ones_e[:], 1.0).then_inc(consts, 1)

            def v_group(G):
                b, g = G // GB, G % GB
                pool.wait_ge(v_r, b + 1)
                pool.wait_ge(vpad_r, 2)
                if G >= 2:
                    pool.wait_ge(pv_done, TT * (G - 1))
                pool.tensor_copy(vcur[G % 2][:, :, :, 0:S],
                                 v_all[:, b * TT:(b + 1) * TT, HG * S * g:HG * S * (g + 1)]
                                 .rearrange("p k (h s) -> p k h s", h=HG)).then_inc(vcur_r, 1)

            def part_3(n, c):
                pool.wait_ge(part2[n], c + 1)
                pool.tensor_tensor(parts[n][:, 2, :], rest[n][:], parts[n][:, 1, :], ALU.subtract).then_inc(part3[n], 1)

            def gates():
                pool.wait_ge(row_r, 4)
                for row in (ga_row, gb_row):
                    r = row.rearrange("p b e -> p (b e)")
                    link(pool.tensor_scalar(gsign[:], r, 0.0, 2.0, ALU.is_ge, ALU.mult))
                    link(pool.tensor_scalar(gsign[:], gsign[:], 1.0, -1.0, ALU.mult, ALU.add))
                    link(pool.tensor_tensor(gabs[:], gsign[:], r, ALU.mult))
                    link(pool.tensor_scalar(gabs[:], gabs[:], 0.25, None, ALU.max))
                    link(pool.tensor_tensor(r, gsign[:], gabs[:], ALU.mult))
                r = cb_row.rearrange("p b e -> p (b e)")
                link(pool.tensor_scalar(r, r, 1.0, 1.0, ALU.mult, ALU.add))
                pool.sem_inc(gate_r, 1)

            def bias_x(d):
                pool.wait_ge(wc_in, 48)
                pool.wait_ge(gate_r, 1)
                link(pool.tensor_tensor(gabo[:], ga_row[:, d, :], bob[:], ALU.mult))
                xd = x_all[:, d * TT:(d + 1) * TT, :]
                link(pool.tensor_tensor(xd, xd, gabo[:].rearrange("p (o e) -> p o e", o=1).broadcast_to((P, TT, E)), ALU.add))

            def residual(d):
                pool.wait_ge(ytmp_r, d + 1)
                xd = x_all[:, d * TT:(d + 1) * TT, :]
                link(pool.tensor_tensor(xd, xd, ytmp[:], ALU.add))
                pool.sem_inc(x2_r, 1)

            def norm2(d):
                if d:
                    pool.wait_ge(ent_w[(d - 1) % 2], 16 * 2 * TT * ((d + 1) // 2))
                    pool.wait_ge(h2T_ps, d)
                layer_norm(x_all, d, stat2_r, d + 1, xn2, None)
                bc = (P, TT, E)
                link(pool.tensor_tensor(xn2[:], xn2[:], cb_row[:, d:d + 1, :].broadcast_to(bc), ALU.mult))
                pool.tensor_tensor(h2, xn2[:], sb_row[:, d:d + 1, :].broadcast_to(bc), ALU.add).then_inc(h2_r, 1)
                pool.tensor_tensor(h2c[:, 1, :, 0:E], xn2[:], sb_row[:, d:d + 1, :].broadcast_to(bc), ALU.add
                                   ).then_inc(h2b_r, 1)

            def enter(d, k):
                if k == 0:
                    pool.wait_ge(pos_r, d + 1)
                    pool.wait_ge(h2b_r, min(d + 1, B - 1))
                n, t = k // TT, k % TT
                pool.indirect_dma_start(
                    slots_scr, bass.IndirectOffsetOnAxis(ap=pos[d % 2][:, k:k + 1], axis=0),
                    h2c[:, n, t, :], None).then_inc(ent_w[d % 2], 16)

            def scatter_y(i):
                pool.wait_ge(yb_r, i + 1)
                pool.wait_ge(dest_r, i + 1)
                pool.indirect_dma_start(y_scr, bass.IndirectOffsetOnAxis(ap=dest[:, i:i + 1], axis=0), yb[i % XR][:],
                                        None, bounds_check=2 * TOK - 1, oob_is_err=False).then_inc(y_w[i % XR], 16)

            norm1(1)
            for G in range(-2, GROUPS):
                b, g = G // GB, G % GB
                if g == 0 and G >= 0 and b + 1 < B:
                    part_3(1, b + 1)
                if G + 1 < GROUPS and G >= -1:
                    v_group(G + 1)
                if G == 0:
                    gates()
                if g == 0 and G >= 0 and b + 2 < B:
                    norm1(b + 2)
                if g == 0 and b >= 1:
                    bias_x(b - 1)
                if G == GROUPS - 3:
                    bias_x(B - 1)
                    pool.sem_inc(bias_r, 1)
                if g == 1 and b >= 1:
                    residual(b - 1)
                    norm2(b - 1)
                if g == 3 and b >= 1:
                    for k in range(2 * TT):
                        enter(b - 1, k)
                if g == 3 and b + 2 < B:
                    part_3(0, b + 2)
            pool.wait_ge(stat2_r, B)
            pool.tensor_tensor(rstd[:], vareps[:], mhalf[:], ALU.pow).then_inc(rstd_r, 1)
            for i in range(ENTER_AT):
                scatter_y(i)
            for k in range(2 * TT):
                enter(B - 1, k)
            for i in range(ENTER_AT, BLOCKS):
                scatter_y(i)
            pool.wait_ge(y_in[POOL_BATCH], 16)
            link(pool.tensor_tensor(y_of(POOL_BATCH, 0), y_of(POOL_BATCH, 0), y_of(POOL_BATCH, 1), ALU.add))
            gated_sum(pool, link, POOL_BATCH).then_inc(fin_r[POOL_BATCH], 1)

        @block.scalar
        def _(act):
            act.wait_ge(c_in, 16)
            act.activation(sig[:], ctb[:], ACT.Exp, scale=-1.0).then_inc(sig_r, 1)

            def modulate(c):
                act.wait_ge(xnT_ps, c + 1)
                if c:
                    act.wait_ge(v_ps, c)
                act.activation(hT[:], tr_flat, ACT.Identity, scale=modc[:, 1, c:c + 1],
                               bias=modc[:, 0, c:c + 1]).then_inc(hT_r, 1)

            def first_part(n, c, src):
                act.wait_ge(qk_ps[n], c + 1)
                if c:
                    act.wait_ge(scr_w[n], 16 * PARTS * c)
                act.copy(parts[n][:, 0, :], src).then_inc(part1[n], 1)

            def second_part(n, c):
                act.wait_ge(rest_r[n], c + 1)
                act.copy(parts[n][:, 1, :], rest[n][:]).then_inc(part2[n], 1)

            def v_copy(c, src):
                act.wait_ge(v_ps, c + 1)
                act.copy(v_all[:, c * TT:(c + 1) * TT, :].rearrange("p t e -> p (t e)"), src).then_inc(v_r, 1)

            def m_rows(G):
                act.wait_ge(mT_ps, G + 1)
                if G >= 2:
                    act.wait_ge(ldm[(G - 2) % RING], 16 * ((G - 2) // GB + 1))
                act.copy(mrow[G % 2][:], tr_m[0:PARTS * NS, 0:P]).then_inc(mrow_r, 1)

            def o_copy(G):
                act.wait_ge(pv_done, TT * (G + 1))
                if G >= 1:
                    act.wait_ge(oT_ps, G)
                act.copy(o_sb[:], pv[:]).then_inc(o_r, 1)

            def a_copy(d):
                act.wait_ge(aT_ps, d + 1)
                if d:
                    act.wait_ge(y_ps, d)
                act.copy(aT[:], tr_flat).then_inc(aT_r, 1)

            def h2_copy(d):
                act.wait_ge(h2T_ps, d + 1)
                if d:
                    act.wait_ge(lg_ps, d)
                act.copy(h2T[:], tr_flat).then_inc(h2T_r, 1)

            def top_exp(d):
                act.wait_ge(top_r, d + 1)
                act.activation(wexp[:], wexp[:], ACT.Exp).then_inc(wexp_r, 1)

            act.wait_ge(mod_r, 1)
            modulate(0)
            for n in range(2):
                first_part(n, 0, mx[n][:, 0, :])
            for n in range(2):
                second_part(n, 0)
            v_copy(0, sc[0][:])
            act.wait_ge(row_ps, 1)
            for n, bank in enumerate((mx[0][:, 1, :], mx[1][:, 1, :], sc[1][:], pv[:])):
                act.copy(mod_row[:, n].rearrange("p b e -> p (b e)"), bank).then_inc(row_r, 1)

            take_act = {"xnT": modulate, "q": lambda c: first_part(0, c, tr_flat), "k": lambda c: first_part(1, c, tr_flat),
                        "v": lambda c: v_copy(c, tr_flat), "m": m_rows, "aT": a_copy, "h2T": h2_copy}

            def exp(G, n):
                kt, j = n // HG, n % HG
                act.wait_ge(sc_ready, NS * G + n + 1)
                if G >= 1 and j == 0:
                    act.wait_ge(pv_done, TT * (G - 1) + kt + 1)
                act.activation(probs[:, kt, j, :], score_bank(NS * G + n)[0], ACT.Exp, scale=EXP_SCALE).then_inc(p_ready, 1)

            for G in range(-2, GROUPS):
                b, g = G // GB, G % GB
                for s in range(UNITS):
                    if G >= 0:
                        exp(G, 2 * s)
                        exp(G, 2 * s + 1)
                    if s == 0 and G >= 1:
                        o_copy(G - 1)
                    for kind, n in extras(G, s):
                        if kind in take_act:
                            take_act[kind](n)
                    if g == 3 and s == 4 and b + 2 < B:
                        second_part(0, b + 2)
                    if g == 3 and s == 7 and b + 2 < B:
                        second_part(1, b + 2)
                    if g == 2 and s == 3 and b >= 1:
                        top_exp(b - 1)
            o_copy(GROUPS - 1)

            def gelu(i):
                act.wait_ge(h_ps, i + 1)
                if i >= 2:
                    act.wait_ge(yb_ps, i - 1)
                for f in range(FC):
                    last = act.activation(g_sb[i % 2][:, P * f:P * (f + 1)], mx[0][:, i % 2, P * f:P * (f + 1)],
                                          ACT.Gelu, bias=w1_blk[i % WR][:, FF + f:FF + f + 1])
                last.then_inc(g_r, 1)

            def weigh_y(i):
                act.wait_ge(yc_r, i + 1)
                if i >= XR:
                    act.wait_ge(y_w[i % XR], 16 * (i // XR))
                act.activation(yb[i % XR][:], yc[i % 2][:], ACT.Copy, scale=xb[i % XR][:, E + 1:E + 2]).then_inc(yb_r, 1)

            for i in range(BLOCKS + 1):
                if LAST.get(i) in take_act:
                    take_act[LAST[i]](B - 1)
                if LAST.get(i) == "px":
                    top_exp(B - 1)
                if i < BLOCKS:
                    gelu(i)
                if i > 0:
                    weigh_y(i - 1)

        @block.vector
        def _(dve):
            chain = [0]

            def link(ins, n=1):
                chain[0] += n
                ins.then_inc(dchain, 1)
                dve.wait_ge(dchain, chain[0])

            def mean_var(src, b, done):
                for t in range(TT - 1):
                    dve.bn_stats(stats[:, t, :], src[:, b * TT + t, :]).then_inc(dchain, 1)
                link(dve.bn_stats(stats[:, TT - 1, :], src[:, b * TT + TT - 1, :]), TT)
                for t in range(TT - 1):
                    dve.bn_aggr(mv[:, t, :], stats[:, t, :]).then_inc(dchain, 1)
                link(dve.bn_aggr(mv[:, TT - 1, :], stats[:, TT - 1, :]), TT)
                dve.tensor_scalar(vareps[:], mv[:, :, 1], EPS, None, ALU.add).then_inc(done, 1)

            def pad_ring(r):
                dve.memset(ks[r][64:96].rearrange("p h t -> p (h t)").bitcast(F32), 0.0)
                dve.memset(ks[r][96:128].rearrange("p h t -> p (h t)").bitcast(F32), ONES_PAIR)
                dve.memset(qs[r][64:128].rearrange("p h t -> p (h t)").bitcast(F32), 0.0).then_inc(pads_r[r], 1)

            pad_ring(0)
            dve.wait_ge(x_in[0], 16)
            mean_var(x_all, 0, stat_r)
            dve.wait_ge(sig_r, 1)
            link(dve.tensor_scalar(sig[:], sig[:], 1.0, None, ALU.add))
            link(dve.reciprocal(sig[:], sig[:]))
            link(dve.tensor_tensor(silu[:], sig[:], ctb[:], ALU.mult))
            dve.sem_inc(silu_r, 1)
            dve.wait_ge(rstd0_r, 1)
            bc = (P, TT, E)
            link(dve.tensor_tensor(xn[:], x_all[:, 0:TT, :], mv[:, :, 0:1].broadcast_to(bc), ALU.subtract))
            dve.tensor_tensor(xn[:], xn[:], rstd[:].rearrange("p (t o) -> p t o", o=1).broadcast_to(bc),
                              ALU.mult).then_inc(xn_r, 1)
            dve.wait_ge(mod_ps, 1)
            link(dve.tensor_copy(modc[:], pv[:, 0:2 * B].rearrange("p (m b) -> p m b", b=B)))
            link(dve.tensor_scalar(modc[:, 1, :], modc[:, 1, :], 1.0, None, ALU.add))
            dve.sem_inc(mod_r, 1)
            dve.tensor_copy(silu_w[:], silu[:].rearrange("p (b o) -> p b o", o=1).broadcast_to((P, B, P))
                            ).then_inc(silu_r, 1)
            pad_ring(1)

            def rest_part(n, c, src):
                dve.wait_ge(part1[n], c + 1)
                if c:
                    dve.wait_ge(part3[n], c)
                link(dve.tensor_tensor(rest[n][:], src, parts[n][:, 0, :], ALU.subtract))
                dve.sem_inc(rest_r[n], 1)

            for n in range(2):
                rest_part(n, 0, mx[n][:, 0, :])
            for n in range(2):
                dve.wait_ge(part2[n], 1)
                dve.tensor_tensor(parts[n][:, 2, :], rest[n][:], parts[n][:, 1, :], ALU.subtract).then_inc(part3[n], 1)

            def make_pads():
                link(dve.memset(capped[:], 0.0))
                link(dve.memset(taken[:], 0.0))
                link(dve.memset(pads[:], 0.0))
                dve.memset(pads[:, E:E + 1], float(PAD)).then_inc(tabz, 1)

            def max_unit(G, u):
                dve.wait_ge(mx_ready, UNITS * G + u + 1)
                if u == 0 and G >= 1:
                    dve.wait_ge(mneg_r, G)
                dve.tensor_reduce(mcol[:, 2 * u:2 * u + 2], mx[u % 2][:], AX_X, ALU.max).then_inc(mx_used, 1)

            def max_split(G):
                dve.wait_ge(mx_used, UNITS * (G + 1))
                if G >= 2:
                    dve.wait_ge(mT_ps, G - 1)
                m = mneg[G % 2]
                link(dve.tensor_scalar(m[:, 0, :], mcol[:], -1.0, None, ALU.mult))
                link(dve.scalar_tensor_tensor(mres[:], mcol[:], -1.0, m[:, 0, :], ALU.mult, ALU.subtract))
                link(dve.tensor_copy(m[:, 1, :], mres[:]))
                dve.tensor_tensor(m[:, 2, :], mres[:], m[:, 1, :], ALU.subtract).then_inc(mneg_r, 1)

            def normalise(G):
                b, g = G // GB, G % GB
                dve.wait_ge(oT_ps, G + 1)
                o = tr[:].rearrange("p q (h c) -> p q h c", c=32)
                rd = rden[:].rearrange("p q (h o) -> p q h o", o=1)
                link(dve.reciprocal(rd, o[:, :, :, S:S + 1]))
                dst = attn[:, b * TT:(b + 1) * TT, HG * S * g:HG * S * (g + 1)].rearrange("p q (h s) -> p q h s", s=S)
                dve.tensor_tensor(dst, o[:, :, :, 0:S], rd.broadcast_to((P, TT, HG, S)), ALU.mult).then_inc(attn_r, 1)

            def gate_y(d):
                dve.wait_ge(y_ps, d + 1)
                dve.wait_ge(gate_r, 1)
                if d:
                    dve.wait_ge(x2_r, d)
                dve.tensor_tensor(ytmp[:], tr[:], ga_row[:, d:d + 1, :].broadcast_to((P, TT, E)),
                                  ALU.mult).then_inc(ytmp_r, 1)

            def stats_2(d):
                dve.wait_ge(x2_r, d + 1)
                dve.wait_ge(xn_r, B)
                if d:
                    dve.wait_ge(h2_r, d)
                mean_var(x_all, d, stat2_r)

            def stats_1(c):
                dve.wait_ge(x_in[c], 16)
                dve.wait_ge(xn_r, c)
                mean_var(x_all, c, stat_r)

            def choose(d):
                dve.wait_ge(lg_ps, d + 1)
                dve.wait_ge(consts, 10)
                link(dve.tensor_copy(logits[:], tr_flat[:, 0:TT * NX].rearrange("p (t e) -> p t e", e=NX)))
                dve.sem_inc(lg_r, 1)
                for t in range(TT):
                    ins = dve.max(top[:, t, :], logits[:, t, :])
                    link(ins, 1) if t == TT - 1 else ins.then_inc(dchain, 1)
                    if t < TT - 1:
                        chain[0] += 1
                for t in range(TT):
                    ins = dve.max_index(topi[:, t, :], top[:, t, :], logits[:, t, :])
                    link(ins, 1) if t == TT - 1 else ins.then_inc(dchain, 1)
                    if t < TT - 1:
                        chain[0] += 1
                dve.tensor_tensor(wexp[:], top[:, :, 1], top[:, :, 0], ALU.subtract).then_inc(top_r, 1)
                link(dve.tensor_copy(topf[:], topi[:, :, 0:2].rearrange("p t n -> p n t")))
                for n in range(2):
                    ins = dve.tensor_tensor(hot[:, n], iota_e[:].rearrange("p (o e) -> p o e", o=1).broadcast_to((P, TT, NX)),
                                            topf[:, n, :].rearrange("p (t o) -> p t o", o=1).broadcast_to((P, TT, NX)),
                                            ALU.is_equal)
                    if n:
                        link(ins)
                    else:
                        chain[0] += 1
                        ins.then_inc(dchain, 1)
                if d:
                    dve.wait_ge(px_ps, d)
                dve.tensor_tensor(hots[:], hot[:, 0], hot[:, 1], ALU.add).then_inc(hot_r, 1)

            def weights(d):
                dve.wait_ge(wexp_r, d + 1)
                dve.wait_ge(h2_r, d + 1)
                if d:
                    dve.wait_ge(ent_w[(d - 1) % 2], 16 * 2 * TT * ((d + 1) // 2))
                w = [h2c[:, n, :, E + 1] for n in range(2)]
                link(dve.tensor_scalar(wden[:], wexp[:], 1.0, None, ALU.add))
                link(dve.reciprocal(w[0], wden[:]))
                link(dve.tensor_tensor(w[1], wexp[:], w[0], ALU.mult))
                link(dve.tensor_copy(h2c[:, :, :, E], tok_id[:, :, d * TT:(d + 1) * TT]))
                if d == B - 1:
                    link(dve.tensor_copy(h2c[:, 1, :, 0:E], h2))

            def place(d):
                dve.wait_ge(px_ps, d + 1)
                link(dve.tensor_copy(ranks[:], tr_flat[:, 0:2 * TT * NX]))
                dve.sem_inc(px_r, 1)
                if d == 0:
                    link(dve.tensor_copy(run[:, 0, :], base_e[:]))
                else:
                    link(dve.tensor_copy(run[:, 0, :], run[:, TT, :]))
                for t in range(TT):
                    link(dve.tensor_tensor(run[:, t + 1, :], ranks[:, (TT + t) * NX:(TT + t + 1) * NX], run[:, t, :], ALU.add))
                link(dve.tensor_tensor(slots[:], ranks[:, 0:TT * NX].rearrange("p (t e) -> p t e", e=NX), run[:, 0:TT, :], ALU.add))
                for n in range(2):
                    link(dve.tensor_tensor(hslots[:, n * TT:(n + 1) * TT, :], hot[:, n], slots[:], ALU.mult))
                link(dve.tensor_reduce(posf[:], hslots[:], AX_X, ALU.add))
                if d >= 2:
                    dve.wait_ge(ent_w[d % 2], 16 * 2 * TT * (d // 2))
                link(dve.tensor_copy(pos[d % 2][:], posf[:]))

            def list_blocks(r, step):
                (count_blocks, pass_experts, first_slots)[step](r)

            def count_blocks(r):
                if r == 1:
                    dve.tensor_copy(end_u[:], run[:, TT, :]).then_inc(end_r, 1)
                link(dve.tensor_tensor(cnt[:], run[:, TT, :], base_e[:], ALU.subtract))
                link(dve.tensor_scalar(cntu[:], cnt[:], float((P - 1) * r), None, ALU.add))
                link(dve.tensor_scalar(cntu[:], cntu[:], 7, None, ALU.logical_shift_right))
                link(dve.tensor_copy(nblk[:], cntu[:]))
                if r == 1:
                    link(dve.tensor_tensor(nblk[:], nblk[:], taken[:, 0:NX], ALU.subtract))
                link(dve.tensor_tensor_scan(cum[:], ones_e[:], nblk[:], 0.0, ALU.mult, ALU.add))

            def pass_experts(r):
                link(dve.tensor_scalar(skip[:], nblk[:], -1.0, float(REGION), ALU.mult, ALU.add))
                if r == 1:
                    link(dve.tensor_tensor(skip[:], skip[:], taken[:, 1:NX + 1], ALU.add))
                    link(dve.tensor_tensor(skip[:], skip[:], taken[:, 0:NX], ALU.subtract))
                a, n = PART[r].start, len(PART[r])
                shape = (P, n, NX)
                link(dve.tensor_tensor(over[:, 0:n], iota_b[:, 0:n].rearrange("p (i o) -> p i o", o=1).broadcast_to(shape),
                                       cum[:].rearrange("p (o e) -> p o e", o=1).broadcast_to(shape), ALU.is_ge))
                link(dve.tensor_reduce(eidf[:, 0:n], over[:, 0:n], AX_X, ALU.add))
                dve.tensor_scalar(eid[:, a:a + n], eidf[:, 0:n], float(NX - 1), None, ALU.min).then_inc(eid_r, 1)

            def first_slots(r):
                a, n = PART[r].start, len(PART[r])
                link(dve.tensor_tensor(over[:, 0:n], over[:, 0:n],
                                       skip[:].rearrange("p (o e) -> p o e", o=1).broadcast_to((P, n, NX)), ALU.mult))
                link(dve.tensor_reduce(startf[:, 0:n], over[:, 0:n], AX_X, ALU.add))
                link(dve.tensor_tensor(startf[:, 0:n], startf[:, 0:n], iota_b[:, 0:n], ALU.add))
                if r == 1:
                    link(dve.tensor_scalar(startf[:, 0:n], startf[:, 0:n], taken[:, 0:1], None, ALU.add))
                link(dve.tensor_scalar(startf[:, 0:n], startf[:, 0:n], float(NX * REGION), float(P), ALU.min, ALU.mult))
                dve.tensor_copy(startu[:, a:a + n], startf[:, 0:n]).then_inc(start_r, 1)
                if r == 0:
                    link(dve.tensor_scalar(capped[:, 1:NX + 1], cum[:], float(FULL), None, ALU.min))
                    link(dve.tensor_tensor(taken[:, 0:NX], capped[:, 1:NX + 1], capped[:, 0:NX], ALU.subtract))

            take_dve = {"q": lambda c: rest_part(0, c, tr_flat), "k": lambda c: rest_part(1, c, tr_flat),
                        "o": normalise, "y": gate_y, "lg": choose, "px": place}

            stats_1(1)
            for G in range(-2, GROUPS):
                b, g = G // GB, G % GB
                for s in range(UNITS):
                    todo = [(kind, n) for kind, n in extras(G, s) if kind in take_dve]
                    if s % 2 == 0:
                        for kind, n in todo:
                            take_dve[kind](n)
                    if G + 2 < GROUPS:
                        max_unit(G + 2, s)
                    if s % 2:
                        for kind, n in todo:
                            take_dve[kind](n)
                    if s == 1 and G == -1:
                        make_pads()
                    if s == 1 and g == 0 and G >= 0 and b + 2 < B:
                        stats_1(b + 2)
                    if s == 1 and g == 1 and b >= 1:
                        stats_2(b - 1)
                    if s == 6 and g == 2 and b >= 1:
                        weights(b - 1)
                        dve.sem_inc(pos_r, 1)
                if G + 2 < GROUPS:
                    max_split(G + 2)
                if G == GROUPS - 2:
                    for step in range(3):
                        list_blocks(0, step)
            normalise(GROUPS - 1)

            def keep_x(i):
                dve.wait_ge(xb_in[i % XR], 16 * (i // XR + 1))
                dve.tensor_copy(dest[:, i:i + 1], xb[i % XR][:, E:E + 1]).then_inc(dest_r, 1)
                dve.wait_ge(xbT_ps, i + 1)
                if i >= 2:
                    dve.wait_ge(h_ps, i - 1)
                dve.tensor_copy(xbT[i % 2][:], xp[i % 2]).then_inc(xbT_r, 1)

            def pick_w1(i):
                part = PART[i >= FULL]
                if (i - part.start) % LOADS == 0:
                    load_experts(i, part.stop)
                if i >= WR:
                    dve.wait_ge(g_r, i - WR + 1)
                dve.tensor_copy(w1_blk[i % WR], w1_all[:, bass.ds(expert[i] * WB, WB)]).then_inc(w1_r, 1)

            def load_experts(i, end):
                dve.wait_ge(eid_r, 1 + (i >= FULL))
                n = min(LOADS, end - i)
                _, values = nc.values_load_multi_w_load_instructions(
                    eid[0:1, i:i + n], engines=[mybir.EngineType.DVE], min_val=0, max_val=NX - 1,
                    skip_runtime_bounds_check_because="a block's expert was clamped to 0 .. NX - 1")
                for k in range(n):
                    expert[i + k] = values[k]

            def add_b2(i):
                dve.wait_ge(yb_ps, i + 1)
                if i >= 2:
                    dve.wait_ge(yb_r, i - 1)
                dve.tensor_tensor(yc[i % 2][:], sc[i % 2][:, 0:E], b2_row[:, bass.ds(expert.pop(i) * E, E)],
                                  ALU.add).then_inc(yc_r, 1)

            expert = {}
            def last_batch(i):
                d = B - 1
                xd = x_all[:, d * TT:(d + 1) * TT, :]
                bc = (P, TT, E)
                if i == 1:
                    gate_y(d)
                    dve.wait_ge(ytmp_r, B)
                    dve.wait_ge(bias_r, 1)
                    link(dve.tensor_tensor(xd, xd, ytmp[:], ALU.add))
                if i == 2:
                    dve.wait_ge(h2_r, d)
                    mean_var(x_all, d, stat2_r)
                if i == 3:
                    dve.wait_ge(rstd_r, 1)
                    link(dve.tensor_tensor(xn2[:], xd, mv[:, :, 0:1].broadcast_to(bc), ALU.subtract))
                    link(dve.tensor_tensor(xn2[:], xn2[:], rstd[:].rearrange("p (t o) -> p t o", o=1).broadcast_to(bc), ALU.mult))
                if i == 4:
                    dve.wait_ge(ent_w[(d - 1) % 2], 16 * 2 * TT * ((d + 1) // 2))
                    dve.wait_ge(h2T_ps, d)
                    link(dve.tensor_tensor(xn2[:], xn2[:], cb_row[:, d:d + 1, :].broadcast_to(bc), ALU.mult))
                    dve.tensor_tensor(h2, xn2[:], sb_row[:, d:d + 1, :].broadcast_to(bc), ALU.add).then_inc(h2_r, 1)
                if i == 6:
                    choose(d)
                if i == 7:
                    place(d)
                if i == 8:
                    weights(d)
                    dve.sem_inc(pos_r, 1)
                if i in LIST_AT:
                    list_blocks(1, LIST_AT.index(i))

            dve.wait_ge(we_in, 32 * NX + 16)
            dve.wait_ge(sc_ready, NS * GROUPS)
            pick_w1(0)
            pick_w1(1)
            keep_x(0)
            for i in range(BLOCKS + 1):
                last_batch(i)
                if i + 1 < BLOCKS:
                    keep_x(i + 1)
                if i + 2 < BLOCKS:
                    pick_w1(i + 2)
                if i > 0:
                    add_b2(i - 1)
            for b in range(B):
                if b == POOL_BATCH:
                    continue
                dve.wait_ge(y_in[b], 16)
                link(dve.tensor_tensor(y_of(b, 0), y_of(b, 0), y_of(b, 1), ALU.add))
                gated_sum(dve, link, b).then_inc(fin_r[b], 1)

        @block.tensor
        def _(pe):
            read = {"xnT": hT_r, "q": rest_r[0], "k": rest_r[1], "v": v_r, "m": mrow_r, "o": attn_r, "aT": aT_r,
                    "y": ytmp_r, "h2T": h2T_r, "lg": lg_r, "px": px_r}

            def take(kind, n):
                before_this = turn[(kind, n)]
                for k, m in uses[max(before_this - 2, 0):before_this]:
                    pe.wait_ge(read[k], m + 1)

            pe.wait_ge(silu_r, 1)
            pe.wait_ge(wa_in, 16)
            for m in range(2):
                last = pe.matmul(pv[:, B * m:B * (m + 1)], wmb[:, E * m:E * (m + 1)], silu[:], start=True, stop=True)
            last.then_inc(mod_ps, 1)
            pe.wait_ge(consts, 4)

            def turn_x(c):
                take("xnT", c)
                pe.wait_ge(xn_r, c + 1)
                for t in range(TT):
                    last = pe.transpose(tr[:, t, :], xn[:, t, :], ident[:])
                last.then_inc(xnT_ps, 1)

            def project(n, c, dst):
                pe.wait_ge(hT_r, c + 1)
                pe.matmul(dst, (wqpb, wkpb)[n][:], hT[:], start=True, stop=True).then_inc(qk_ps[n], 1)

            def project_v(c, dst):
                for t in range(TT):
                    last = pe.matmul(dst[:, P * t:P * (t + 1)], hT[:, P * t:P * (t + 1)], wkb[:],
                                     start=True, stop=True)
                last.then_inc(v_ps, 1)

            turn_x(0)
            pe.wait_ge(wb_in, 48)
            for n in range(2):
                project(n, 0, mx[n][:, 0, :])
            project_v(0, sc[0][:])
            pe.wait_ge(mod_r, 1)
            pe.wait_ge(silu_r, 2)
            for m, bank in zip((2, 5, 4, 3), (mx[0][:, 1, :], mx[1][:, 1, :], sc[1][:], pv[:])):
                for b in range(B):
                    last = pe.matmul(bank[:, E * b:E * (b + 1)], silu_w[:, b, :], wmb[:, E * m:E * (m + 1)],
                                     start=True, stop=True)
            last.then_inc(row_ps, 1)

            def maxima(G, n):
                b, g = G // GB, G % GB
                u, c = n // 2, n % 2
                if n == 0:
                    pe.wait_ge(ld[g], LDG * (b + 1))
                if c == 0 and UNITS * G + u >= 2:
                    pe.wait_ge(mx_used, UNITS * G + u - 1)
                j, qt = n // TT, n % TT
                ins = pe.matmul(mx[u % 2][:, c, :], qs[g][0:MROW, j, P * qt:P * (qt + 1)],
                                ks[g][0:MROW, j, :], start=True, stop=True)
                if c == 1:
                    ins.then_inc(mx_ready, 1)

            def score(G, n):
                b, g = G // GB, G % GB
                kt, j = n // HG, n % HG
                if n == 0:
                    pe.wait_ge(ldm[g], 16 * (b + 1))
                bank, banks = score_bank(NS * G + n)
                if NS * G + n >= banks:
                    pe.wait_ge(p_ready, NS * G + n - banks + 1)
                if NS * G + n == FREE + 2:
                    pe.wait_ge(mx_used, UNITS * GROUPS)
                pe.matmul(bank, ks[g][0:KEXP, j, P * kt:P * (kt + 1)], qs[g][0:KEXP, j, :],
                          start=True, stop=True).then_inc(sc_ready, 1)

            def weigh(G, kt):
                pe.wait_ge(p_ready, NS * G + HG * (kt + 1))
                if kt == 0:
                    pe.wait_ge(vcur_r, G + 1)
                    if G:
                        pe.wait_ge(o_r, G)
                for j in range(HG):
                    last = pe.matmul(pv[32 * j:32 * (j + 1), :], vcur[G % 2][:, kt, j, :], probs[:, kt, j, :],
                                     start=kt == 0, stop=kt == TT - 1, skip_group_check=True)
                last.then_inc(pv_done, 1)

            def turn_max(G):
                take("m", G)
                pe.wait_ge(mneg_r, G + 1)
                pe.transpose(tr_m[0:PARTS * NS, 0:P], mneg[G % 2][:].rearrange("p i n -> p (i n)"),
                             identb[:]).then_inc(mT_ps, 1)

            def turn_out(G):
                take("o", G)
                pe.wait_ge(o_r, G + 1)
                for t in range(TT):
                    last = pe.transpose(tr[:, t, :], o_sb[:, P * t:P * (t + 1)], ident[:])
                last.then_inc(oT_ps, 1)

            def turn_attn(d):
                take("aT", d)
                pe.wait_ge(attn_r, GB * (d + 1))
                for t in range(TT):
                    last = pe.transpose(tr[:, t, :], attn[:, d * TT + t, :], ident[:])
                last.then_inc(aT_ps, 1)

            def out_proj(d):
                take("y", d)
                pe.wait_ge(aT_r, d + 1)
                pe.wait_ge(wc_in, 48)
                for t in range(TT):
                    last = pe.matmul(tr[:, t, :], aT[:, P * t:P * (t + 1)], wob[:], start=True, stop=True)
                last.then_inc(y_ps, 1)

            def turn_h2(d):
                take("h2T", d)
                pe.wait_ge(h2_r, d + 1)
                for t in range(TT):
                    last = pe.transpose(tr[:, t, :], h2[:, t, :], ident[:])
                last.then_inc(h2T_ps, 1)

            def route(d):
                take("lg", d)
                pe.wait_ge(h2T_r, d + 1)
                for t in range(TT):
                    last = pe.matmul(tr_flat[:, NX * t:NX * (t + 1)], h2T[:, P * t:P * (t + 1)], rwb[:],
                                     start=True, stop=True)
                last.then_inc(lg_ps, 1)

            def rank(d):
                take("px", d)
                pe.wait_ge(hot_r, d + 1)
                pe.wait_ge(consts, 6)
                h = hots[:].rearrange("p t e -> p (t e)")
                pe.matmul(tr_flat[:, 0:TT * NX], before[:], h, start=True, stop=True)
                pe.matmul(tr_flat[:, TT * NX:2 * TT * NX], onesb[:], h, start=True, stop=True).then_inc(px_ps, 1)

            work = {"xnT": turn_x, "q": lambda c: (take("q", c), project(0, c, tr_flat)),
                    "k": lambda c: (take("k", c), project(1, c, tr_flat)),
                    "v": lambda c: (take("v", c), project_v(c, tr_flat)),
                    "m": turn_max, "o": turn_out,
                    "aT": turn_attn, "y": out_proj, "h2T": turn_h2, "lg": route, "px": rank}

            pe.wait_ge(row_r, 4)
            pe.wait_ge(v_r, 1)
            for n in range(2):
                pe.wait_ge(rest_r[n], 1)
            for G in range(-2, GROUPS):
                for p in range(TT):
                    if G >= 0:
                        score(G, 4 * p)
                        score(G, 4 * p + 1)
                        if NS * G + 4 * p >= FREE:
                            score(G, 4 * p + 2)
                            score(G, 4 * p + 3)
                        if p == 0 and G >= 1:
                            weigh(G - 1, TT - 1)
                        if p >= 1:
                            weigh(G, p - 1)
                    for kind, n in extras(G, 2 * p):
                        work[kind](n)
                    if G >= 0 and NS * G + 4 * p < FREE:
                        score(G, 4 * p + 2)
                    if G + 2 < GROUPS:
                        maxima(G + 2, 4 * p)
                    if G >= 0 and NS * G + 4 * p < FREE:
                        score(G, 4 * p + 3)
                    if G + 2 < GROUPS:
                        for n in range(1, 4):
                            maxima(G + 2, 4 * p + n)
                    for kind, n in extras(G, 2 * p + 1):
                        work[kind](n)
            weigh(GROUPS - 1, TT - 1)
            turn_out(GROUPS - 1)

            pe.wait_ge(eid_r, 1)
            pe.wait_ge(we_in, 32 * NX + 16)
            def turn_block(i):
                pe.wait_ge(xb_in[i % XR], 16 * (i // XR + 1))
                if i >= 2:
                    pe.wait_ge(xbT_r, i - 1)
                pe.transpose(xp[i % 2], xb[i % XR][:, 0:E], ident[:]).then_inc(xbT_ps, 1)

            def experts_from(i, end):
                pe.wait_ge(eid_r, 1 + (i >= FULL))
                n = min(LOADS, end - i)
                _, values = nc.values_load_multi_w_load_instructions(
                    eid[0:1, i:i + n], engines=[mybir.EngineType.PE], min_val=0, max_val=NX - 1,
                    skip_runtime_bounds_check_because="DVE clamps a block's expert to 0 .. NX - 1")
                for k in range(n):
                    expert[i + k] = values[k]

            def expand(i):
                pe.wait_ge(xbT_r, i + 1)
                pe.wait_ge(w1_r, i + 1)
                if i >= 2:
                    pe.wait_ge(g_r, i - 1)
                for f in range(FC):
                    last = pe.matmul(mx[0][:, i % 2, P * f:P * (f + 1)], w1_blk[i % WR][:, P * f:P * (f + 1)],
                                     xbT[i % 2][:], start=True, stop=True)
                last.then_inc(h_ps, 1)

            def contract(i, e):
                pe.wait_ge(g_r, i + 1)
                if i >= 2:
                    pe.wait_ge(yc_r, i - 1)
                y = sc[i % 2][:, 0:E]
                for f in range(FC):
                    last = pe.matmul(y, g_sb[i % 2][:, P * f:P * (f + 1)], w2_all[:, bass.ds(e * (FC * E) + f * E, E)],
                                     start=f == 0, stop=f == FC - 1)
                last.then_inc(yb_ps, 1)

            expert = {}
            turn_block(0)
            for i in range(BLOCKS + 1):
                if i in LAST:
                    work[LAST[i]](B - 1)
                if i < BLOCKS:
                    part = PART[i >= FULL]
                    if (i - part.start) % LOADS == 0:
                        experts_from(i, part.stop)
                    expand(i)
                if i + 1 < BLOCKS:
                    turn_block(i + 1)
                if i > 0:
                    contract(i - 1, expert.pop(i - 1))


_ARGS = ["x", "cT", "wk", "wqp", "wkp", "wo", "bo", "router_wT", "w1b", "w2T", "b2", "wmod"]


def kernel(L0_attn_x, L0_attn_Wk, L0_attn_Wq, L0_attn_Wo, L0_attn_bo, L0_ffn_router_w, L0_ffn_w1,
           L0_ffn_b1, L0_ffn_w2, L0_ffn_b2, L0_c, L0_wmod):
    import numpy as np
    import concourse.bacc as bacc
    from concourse.bass_utils import run_bass_kernel_spmd

    n_x, ff, e = L0_ffn_w1.shape
    w1 = np.asarray(L0_ffn_w1)
    w2 = np.asarray(L0_ffn_w2)

    def by_group(w):
        return np.asarray(w).reshape(e, HEADS // HG, HG, e // HEADS).transpose(0, 1, 3, 2).reshape(e, e)

    laid = {
        "x": np.asarray(L0_attn_x),
        "cT": np.asarray(L0_c).T,
        "wk": np.asarray(L0_attn_Wk), "wo": np.asarray(L0_attn_Wo),
        "wqp": by_group(L0_attn_Wq), "wkp": by_group(L0_attn_Wk),
        "bo": np.asarray(L0_attn_bo).reshape(1, e),
        "router_wT": np.asarray(L0_ffn_router_w).T,
        "w1b": np.concatenate([w1.transpose(2, 0, 1),
                               np.asarray(L0_ffn_b1).reshape(n_x, ff // 128, 128).transpose(2, 0, 1)], 2)
                 .reshape(e, -1),
        "w2T": w2.transpose(0, 2, 1).reshape(n_x, ff // 128, 128, e).transpose(2, 0, 1, 3)
                 .reshape(128, n_x * ff // 128 * e),
        "b2": np.asarray(L0_ffn_b2).reshape(1, n_x * e),
        "wmod": np.asarray(L0_wmod),
    }
    laid = {k: np.ascontiguousarray(v) for k, v in laid.items()}
    nc = bacc.Bacc("TRN2", target_bir_lowering=False, num_devices=1)
    aps = [nc.dram_tensor(f"in_{k}", laid[k].shape, mybir.dt.from_np(laid[k].dtype), kind="ExternalInput").ap()
           for k in _ARGS]
    out = nc.dram_tensor("out_x", laid["x"].shape, F32, kind="ExternalOutput").ap()
    build(nc, *aps, out)
    r = run_bass_kernel_spmd(nc, [{f"in_{k}": laid[k] for k in _ARGS}], core_ids=[0])
    return r.results[0]["out_x"]
```
